# Optimizing a Trainium2 kernel written in Bass

```python
import numpy as np
import jax
import jax.numpy as jnp

def _softmax(x, axis=-1):
    return jax.nn.softmax(x, axis=axis)

def _gelu(x):
    return jax.nn.gelu(x, approximate=True)

def _silu(x):
    return jax.nn.silu(x)

def _sigmoid(x):
    return jax.nn.sigmoid(x)

def _layernorm(x, axis=-1, eps=1e-05):
    m = jnp.mean(x, axis=axis, keepdims=True)
    v = jnp.var(x, axis=axis, keepdims=True)
    return (x - m) / jnp.sqrt(v + eps)

def _scatter_add(tgt, idx, src, axis=0):
    return tgt.at[idx].add(src)

def _segment_sum(src, seg, n):
    return jax.ops.segment_sum(src, seg, n)
kernel_name = 'mk_adaln_attn_ffn_d1_seqx_r8_91f478'

def setup_inputs(seed: int=0):
    np.random.seed(seed)
    _w = jnp.asarray

    def _rec_inputs():
        import jax
        import jax.numpy as jnp
        _rk = jax.random.key(seed)
        x = -0.000125 + 0.9999 * jax.random.normal(jax.random.fold_in(_rk, 1), (128, 32, 512), jnp.float32)
        _lenS = 32 - jax.random.randint(jax.random.fold_in(_rk, 7), (128,), 0, max(1, 32 // 4) + 1, jnp.int32)
        _lenS2 = 32 - jax.random.randint(jax.random.fold_in(_rk, 8), (128,), 0, max(1, 32 // 4) + 1, jnp.int32)
        cond_128 = 0.0061147 + 1.02565 * jax.random.normal(jax.random.fold_in(_rk, 11), (128, 128), jnp.float32)
        fside_S_0 = -0.022604 + 0.987366 * jax.random.normal(jax.random.fold_in(_rk, 12), (32,), jnp.float32)
        return (x, cond_128, fside_S_0)
    x, cond_128, fside_S_0 = _rec_inputs()

    def _L0_cond_setup():
        import jax, jax.numpy as jnp
        import numpy as np
        from jax import lax
        N, C_IN, L = (32, 32, 512)
        C_OUT, K, GROUPS = (32, 9, 4)
        C_DIM, PAD, STRIDE = (128, 4, 1)
        key = jax.random.key(seed)
        k1, k2, k3, k4, k5 = jax.random.split(key, 5)
        x = jax.random.normal(k1, (N, C_IN, L), dtype=jnp.float32)
        c = jax.random.normal(k2, (N, C_DIM), dtype=jnp.float32)
        weight = jax.random.normal(k3, (C_OUT, C_IN // GROUPS, K), dtype=jnp.float32)
        c_weight = jax.random.normal(k4, (C_OUT, C_DIM), dtype=jnp.float32)
        bias = jax.random.normal(k5, (C_OUT,), dtype=jnp.float32)
        return {'x': x, 'c': c, 'weight': weight, 'c_weight': c_weight, 'bias': bias}
    _L0_cond_all = _L0_cond_setup()
    _L0_cond_in = {k: v for k, v in _L0_cond_all.items() if k in ('weight', 'c_weight')}
    del _L0_cond_all

    def _L0_attn_setup():
        import jax, jax.numpy as jnp
        import numpy as np
        HIDDEN = 512
        NH = 32
        NKV = 8
        HD = 128
        GS = 128
        BASE = 10000.0
        B, S = (2, 256)

        def _dequant(codes, scales):
            w = codes.astype(jnp.float32) - 8.0
            return w * jnp.repeat(scales, GS, axis=0)

        def _rope(x):
            s, d = (x.shape[2], x.shape[3])
            pos = jnp.arange(s, dtype=jnp.float32)
            inv_freq = 1.0 / BASE ** (jnp.arange(0, d, 2, dtype=jnp.float32) / d)
            f = pos[:, None] * inv_freq[None, :]
            cos = jnp.cos(f)[None, None]
            sin = jnp.sin(f)[None, None]
            xe = x[..., ::2]
            xo = x[..., 1::2]
            re = xe * cos - xo * sin
            ro = xo * cos + xe * sin
            return jnp.stack([re, ro], axis=-1).reshape(x.shape)
        key = jax.random.key(seed)
        ks = jax.random.split(key, 9)

        def codes(k, i, o):
            return jax.random.randint(k, (i, o), 0, 16, dtype=jnp.int32)

        def scales(k, i, o):
            return jax.random.uniform(k, (i // GS, o), dtype=jnp.float32) * 0.02
        return {'hidden_states': jax.random.normal(ks[0], (B, S, HIDDEN), jnp.float32), 'q_codes': codes(ks[1], HIDDEN, NH * HD), 'q_scales': scales(ks[2], HIDDEN, NH * HD), 'k_codes': codes(ks[3], HIDDEN, NKV * HD), 'k_scales': scales(ks[4], HIDDEN, NKV * HD), 'v_codes': codes(ks[5], HIDDEN, NKV * HD), 'v_scales': scales(ks[6], HIDDEN, NKV * HD), 'o_codes': codes(ks[7], NH * HD, HIDDEN), 'o_scales': scales(ks[8], NH * HD, HIDDEN)}
    _L0_attn_all = _L0_attn_setup()
    _L0_attn_in = {k: v for k, v in _L0_attn_all.items() if k in ('q_codes', 'q_scales', 'k_codes', 'k_scales', 'v_codes', 'v_scales', 'o_codes', 'o_scales')}
    del _L0_attn_all

    def _L0_cond2_setup():
        import jax, jax.numpy as jnp
        import numpy as np
        K = 8
        T = 1.0
        D_EMBD = 128
        IN_C = 32
        OUT_C = 32
        BS = 32
        H = 512
        HID = 128
        key = jax.random.key(seed)
        ks = jax.random.split(key, 10)
        s = lambda fan_in: 1.0 / np.sqrt(fan_in)
        return {'x': jax.random.normal(ks[0], (BS, IN_C, H), dtype=jnp.float32), 'embedding': jax.random.normal(ks[1], (BS, D_EMBD), dtype=jnp.float32), 'W0': jax.random.normal(ks[2], (D_EMBD, HID), dtype=jnp.float32) * s(D_EMBD), 'b0': jnp.zeros((HID,), dtype=jnp.float32), 'W1': jax.random.normal(ks[3], (HID, HID), dtype=jnp.float32) * s(HID), 'b1': jnp.zeros((HID,), dtype=jnp.float32), 'W2': jax.random.normal(ks[4], (HID, K), dtype=jnp.float32) * s(HID), 'b2': jnp.zeros((K,), dtype=jnp.float32), 'weight': jax.random.normal(ks[5], (K, OUT_C, IN_C, 1), dtype=jnp.float32) * s(IN_C), 'bias_k': jax.random.normal(ks[6], (K, OUT_C), dtype=jnp.float32) * 0.1}
    _L0_cond2_all = _L0_cond2_setup()
    _L0_cond2_in = {k: v for k, v in _L0_cond2_all.items() if k in ('W0', 'b0', 'W1', 'b1', 'W2', 'b2', 'weight', 'bias_k')}
    del _L0_cond2_all

    def _L0_ffn_setup():
        import jax, jax.numpy as jnp
        import numpy as np
        N_EXPERTS = 28
        TOP_K = 2
        RANK = 8
        LORA_ALPHA = 16
        SCALING = LORA_ALPHA / RANK
        TEMP = 1.0
        key = jax.random.key(seed)
        ks = jax.random.split(key, 5)
        B, S, D_IN, D_OUT = (4, 256, 512, 512)
        x = jax.random.normal(ks[0], (B, S, D_IN), dtype=jnp.float32)
        base_W = jax.random.normal(ks[1], (D_OUT, D_IN), dtype=jnp.float32) * (1.0 / np.sqrt(D_IN))
        gate_W = jax.random.normal(ks[2], (N_EXPERTS, D_IN), dtype=jnp.float32) * (1.0 / np.sqrt(D_IN))
        lora_A = jax.random.normal(ks[3], (N_EXPERTS, RANK, D_IN), dtype=jnp.float32) * (1.0 / np.sqrt(D_IN))
        lora_B = jax.random.normal(ks[4], (N_EXPERTS, D_OUT, RANK), dtype=jnp.float32) * 0.01
        return {'x': x, 'base_W': base_W, 'gate_W': gate_W, 'lora_A': lora_A, 'lora_B': lora_B}
    _L0_ffn_all = _L0_ffn_setup()
    _L0_ffn_in = {k: v for k, v in _L0_ffn_all.items() if k in ('base_W', 'gate_W', 'lora_A', 'lora_B')}
    del _L0_ffn_all
    return {'x': x, 'cond_128': cond_128, 'fside_S_0': fside_S_0, 'L0_cond_weight': _L0_cond_in['weight'], 'L0_cond_c_weight': _L0_cond_in['c_weight'], 'L0_attn_q_codes': _L0_attn_in['q_codes'], 'L0_attn_q_scales': _L0_attn_in['q_scales'], 'L0_attn_k_codes': _L0_attn_in['k_codes'], 'L0_attn_k_scales': _L0_attn_in['k_scales'], 'L0_attn_v_codes': _L0_attn_in['v_codes'], 'L0_attn_v_scales': _L0_attn_in['v_scales'], 'L0_attn_o_codes': _L0_attn_in['o_codes'], 'L0_attn_o_scales': _L0_attn_in['o_scales'], 'L0_cond2_W0': _L0_cond2_in['W0'], 'L0_cond2_b0': _L0_cond2_in['b0'], 'L0_cond2_W1': _L0_cond2_in['W1'], 'L0_cond2_b1': _L0_cond2_in['b1'], 'L0_cond2_W2': _L0_cond2_in['W2'], 'L0_cond2_b2': _L0_cond2_in['b2'], 'L0_cond2_weight': _L0_cond2_in['weight'], 'L0_cond2_bias_k': _L0_cond2_in['bias_k'], 'L0_ffn_base_W': _L0_ffn_in['base_W'], 'L0_ffn_gate_W': _L0_ffn_in['gate_W'], 'L0_ffn_lora_A': _L0_ffn_in['lora_A'], 'L0_ffn_lora_B': _L0_ffn_in['lora_B']}

def reference(x, cond_128, fside_S_0, L0_cond_weight, L0_cond_c_weight, L0_attn_q_codes, L0_attn_q_scales, L0_attn_k_codes, L0_attn_k_scales, L0_attn_v_codes, L0_attn_v_scales, L0_attn_o_codes, L0_attn_o_scales, L0_cond2_W0, L0_cond2_b0, L0_cond2_W1, L0_cond2_b1, L0_cond2_W2, L0_cond2_b2, L0_cond2_weight, L0_cond2_bias_k, L0_ffn_base_W, L0_ffn_gate_W, L0_ffn_lora_A, L0_ffn_lora_B):
    import jax
    import jax.numpy as jnp

    def _L0_cond_ref(x, c, weight, c_weight, bias):
        import jax, jax.numpy as jnp
        import numpy as np
        from jax import lax
        N, C_IN, L = (32, 32, 512)
        C_OUT, K, GROUPS = (32, 9, 4)
        C_DIM, PAD, STRIDE = (128, 4, 1)
        out = lax.conv_general_dilated(x, weight, window_strides=(STRIDE,), padding=[(PAD, PAD)], dimension_numbers=('NCH', 'OIH', 'NCH'), feature_group_count=GROUPS)
        ctx = jnp.einsum('nd,od->no', c, c_weight)
        out = out + ctx[:, :, None] + bias[None, :, None]
        return out

    def _L0_attn_ref(hidden_states, q_codes, q_scales, k_codes, k_scales, v_codes, v_scales, o_codes, o_scales):
        import jax, jax.numpy as jnp
        import numpy as np
        HIDDEN = 512
        NH = 32
        NKV = 8
        HD = 128
        GS = 128
        BASE = 10000.0
        B, S = (2, 256)

        def _dequant(codes, scales):
            w = codes.astype(jnp.float32) - 8.0
            return w * jnp.repeat(scales, GS, axis=0)

        def _rope(x):
            s, d = (x.shape[2], x.shape[3])
            pos = jnp.arange(s, dtype=jnp.float32)
            inv_freq = 1.0 / BASE ** (jnp.arange(0, d, 2, dtype=jnp.float32) / d)
            f = pos[:, None] * inv_freq[None, :]
            cos = jnp.cos(f)[None, None]
            sin = jnp.sin(f)[None, None]
            xe = x[..., ::2]
            xo = x[..., 1::2]
            re = xe * cos - xo * sin
            ro = xo * cos + xe * sin
            return jnp.stack([re, ro], axis=-1).reshape(x.shape)
        b, s, _ = hidden_states.shape
        q = hidden_states @ _dequant(q_codes, q_scales)
        k = hidden_states @ _dequant(k_codes, k_scales)
        v = hidden_states @ _dequant(v_codes, v_scales)
        q = q.reshape(b, s, NH, HD).transpose(0, 2, 1, 3)
        k = k.reshape(b, s, NKV, HD).transpose(0, 2, 1, 3)
        v = v.reshape(b, s, NKV, HD).transpose(0, 2, 1, 3)
        q = _rope(q)
        k = _rope(k)
        rf = NH // NKV
        k = jnp.repeat(k, rf, axis=1)
        v = jnp.repeat(v, rf, axis=1)
        scale = HD ** (-0.5)
        causal = jnp.tril(jnp.ones((s, s), dtype=bool))
        mask = jnp.where(causal, 0.0, -jnp.inf).astype(q.dtype)
        scores = jnp.einsum('bhqd,bhkd->bhqk', q, k) * scale + mask[None, None]
        attn = jax.nn.softmax(scores, axis=-1)
        out = jnp.einsum('bhqk,bhkd->bhqd', attn, v)
        out = out.transpose(0, 2, 1, 3).reshape(b, s, NH * HD)
        return out @ _dequant(o_codes, o_scales)

    def _L0_cond2_ref(x, embedding, W0, b0, W1, b1, W2, b2, weight, bias_k):
        import jax, jax.numpy as jnp
        import numpy as np
        K = 8
        T = 1.0
        D_EMBD = 128
        IN_C = 32
        OUT_C = 32
        BS = 32
        H = 512
        HID = 128
        h = jax.nn.gelu(embedding @ W0 + b0, approximate=False)
        h = jax.nn.gelu(h @ W1 + b1, approximate=False)
        att = jax.nn.softmax((h @ W2 + b2) / T, axis=-1)
        agg_w = jnp.einsum('bk,koi->boi', att, weight[..., 0])
        agg_b = att @ bias_k
        out = jnp.einsum('boi,bih->boh', agg_w, x) + agg_b[:, :, None]
        return out

    def _L0_ffn_ref(x, base_W, gate_W, lora_A, lora_B):
        import jax, jax.numpy as jnp
        import numpy as np
        N_EXPERTS = 28
        TOP_K = 2
        RANK = 8
        LORA_ALPHA = 16
        SCALING = LORA_ALPHA / RANK
        TEMP = 1.0
        B, S, D_in = x.shape
        xf = x.reshape(B * S, D_in)
        base = xf @ base_W.T
        logits = xf @ gate_W.T
        top_vals, top_idx = jax.lax.top_k(logits, TOP_K)
        top_probs = jax.nn.softmax(top_vals / TEMP, axis=-1)
        N = xf.shape[0]
        gate_full = jnp.zeros((N, N_EXPERTS), dtype=xf.dtype).at[jnp.arange(N)[:, None], top_idx].add(top_probs)
        h = jnp.einsum('nd,erd->ner', xf, lora_A)
        h = h * (gate_full * SCALING)[:, :, None]
        lora_out = jnp.einsum('ner,eor->no', h, lora_B)
        out = base + lora_out
        return out.reshape(B, S, -1)
    x = x + _L0_attn_ref(_L0_cond_ref(x, cond_128, L0_cond_weight, L0_cond_c_weight, fside_S_0), L0_attn_q_codes, L0_attn_q_scales, L0_attn_k_codes, L0_attn_k_scales, L0_attn_v_codes, L0_attn_v_scales, L0_attn_o_codes, L0_attn_o_scales)
    x = x + _L0_ffn_ref(_L0_cond2_ref(x, cond_128, L0_cond2_W0, L0_cond2_b0, L0_cond2_W1, L0_cond2_b1, L0_cond2_W2, L0_cond2_b2, L0_cond2_weight, L0_cond2_bias_k), L0_ffn_base_W, L0_ffn_gate_W, L0_ffn_lora_A, L0_ffn_lora_B)
    return x

_drawn_inputs = setup_inputs


def setup_inputs(seed=0):
    import zlib

    import numpy as np

    out = dict(_drawn_inputs(seed))
    spreads = {'L0_cond2_b0': (0.0, 0.71), 'L0_cond2_b1': (0.0, 0.471), 'L0_cond2_b2': (0.0, 0.1)}
    factors = {'L0_cond2_bias_k': 8.0,
     'L0_ffn_gate_W': 2.774,
     'L0_ffn_lora_A': 3.071,
     'L0_ffn_lora_B': 2.719}
    for name, (base, spread) in spreads.items():
        noise = np.random.default_rng([zlib.crc32(name.encode()), seed]).standard_normal(out[name].shape)
        drawn = base * np.exp(spread * noise) if base else spread * noise
        out[name] = jnp.asarray(drawn.astype(out[name].dtype))
    for name, factor in factors.items():
        out[name] = (out[name] * factor).astype(out[name].dtype)
    return out
```

```python
from contextlib import ExitStack

import concourse.bass as bass
from concourse import mybir

F32 = mybir.dt.float32
F16 = mybir.dt.float16
BF16 = mybir.dt.bfloat16
I32 = mybir.dt.int32
U32 = mybir.dt.uint32
ALU = mybir.AluOpType
ACT = mybir.ActivationFunctionType
AX = mybir.AxisListType

P = 128
B, S, D = 128, 32, 512
TOKENS = B * S
TILES = TOKENS // P
TB = P // S
KT = D // P
CHUNK = 512
CHUNKS = TOKENS // CHUNK
CT = CHUNK // P
NKV, RF, HD = 8, 4, 128
TAPS, PAD, CGROUPS = 9, 4, 4
CG = S // CGROUPS
XP = D + 2 * PAD
WQ, WK, WV, WO = 0, 2048, 2560, 3072
WG = 5120
WSTEP = WG * NKV // TILES
STEPS_G = WG // WSTEP
WSCALE = 256.0
FSCALE = 64.0
SM_SCALE = float(HD) ** -0.5
EXPERTS, RANK, LORA = 28, 8, 2.0
ER = EXPERTS * RANK
EH = ER // 2
GL = EXPERTS + ER
COND_K = 8
PASSES = ((0, 0), (0, 1), (1, 0))


def layer(nc, a, out):
    w_split = nc.dram_tensor("w_split", [P, 2, NKV * WG], F16, kind="Internal").ap()
    ctx_rows = nc.dram_tensor("ctx_rows", [B, S], F32, kind="Internal").ap()
    aggb_rows = nc.dram_tensor("aggb_rows", [B, S], F32, kind="Internal").ap()
    aggw_rows = nc.dram_tensor("aggw_rows", [B, S * S], F32, kind="Internal").ap()
    with ExitStack() as ctx:
        bank = [ctx.enter_context(nc.psum_tensor(f"bank{n}", [P, 512], F32)) for n in range(8)]
        x1 = ctx.enter_context(nc.sbuf_tensor("x1", [P, TILES, D], F32))
        h_ctx = ExitStack()
        hT = h_ctx.enter_context(nc.sbuf_tensor("hT", [P, KT, 2, TOKENS], F16))
        with ExitStack() as c1:
            conv_w = c1.enter_context(nc.sbuf_tensor("conv_w", [P, 2, TAPS, P], F16))
            setup(nc, a, bank, conv_w, ctx_rows, aggb_rows, aggw_rows)
            conv_and_dequant(nc, a, bank, x1, hT, conv_w, ctx_rows, w_split)
        with ExitStack() as c2:
            attention(nc, c2, a, bank, x1, hT, w_split)
        h_ctx.close()
        with ExitStack() as c3:
            mix_and_ffn(nc, c3, a, bank, x1, aggb_rows, aggw_rows, out)


def setup(nc, a, bank, conv_w, ctx_rows, aggb_rows, aggw_rows):
    with ExitStack() as c:
        def sb(name, shape, dt=F32):
            return c.enter_context(nc.sbuf_tensor(name, shape, dt))

        def sem(name):
            return c.enter_context(nc.semaphore(name))

        conv_f = sb("conv_f", [P, TAPS, P])
        cond_T = sb("cond_T", [P, B])
        cw_T = sb("cw_T", [P, S])
        fside = sb("fside", [P, S])
        w0 = sb("w0", [P, P])
        w1 = sb("w1", [P, P])
        w2 = sb("w2", [P, COND_K])
        b0 = sb("b0", [P, 1])
        b1 = sb("b1", [P, 1])
        b2 = sb("b2", [P, COND_K])
        kern = sb("kern", [COND_K, S * S])
        kern_b = sb("kern_b", [COND_K, S])
        ident = sb("ident_s", [P, P])
        ctx_sb = sb("ctx_sb", [P, S])
        hid = sb("hid", [P, 2, B])
        att = sb("att", [P, COND_K])
        att_T = sb("att_T", [COND_K, B])
        stat = sb("stat", [P, 4])
        aggw_sb = sb("aggw_sb", [P, S * S])
        aggb_sb = sb("aggb_sb", [P, S])

        conv_zeroed = sem("conv_zeroed")
        conv_loaded = sem("conv_loaded")
        params_loaded = sem("params_loaded")
        conv_hi = sem("conv_hi")
        conv_lo = sem("conv_lo")
        ctx_psum = sem("ctx_psum")
        ctx_added = sem("ctx_added")
        hid_psum = sem("hid_psum")
        att_max = sem("att_max")
        hid_done = sem("hid_done")
        att_psum = sem("att_psum")
        att_step = sem("att_step")
        att_exp = sem("att_exp")
        att_T_psum = sem("att_T_psum")
        att_T_done = sem("att_T_done")
        agg_psum = sem("agg_psum")
        agg_done = sem("agg_done")
        rows_stored = sem("rows_stored")
        block = c.enter_context(nc.Block())

        @block.sync
        def _(sp):
            for dst, src in ((cond_T, a["cond_T"]), (cw_T, a["cw_T"]), (fside, a["fside"].partition_broadcast(P)),
                             (w0, a["w0"]), (w1, a["w1"]), (w2, a["w2"]), (b0, a["b0"]), (b1, a["b1"]),
                             (b2, a["b2"].partition_broadcast(P)), (kern, a["kern"]), (kern_b, a["kern_b"]),
                             (ident, a["ident"])):
                sp.dma_start(dst[:], src).then_inc(params_loaded, 16)
            sp.wait_ge(ctx_added, 1)
            sp.dma_start(ctx_rows, ctx_sb[:]).then_inc(rows_stored, 16)
            sp.wait_ge(agg_done, 3)
            sp.dma_start(aggw_rows, aggw_sb[:]).then_inc(rows_stored, 16)
            sp.dma_start(aggb_rows, aggb_sb[:]).then_inc(rows_stored, 16)
            sp.wait_ge(rows_stored, 48)

        @block.gpsimd
        def _(pool):
            pool.memset(conv_f[:], 0.0).then_inc(conv_zeroed, 1)

        @block.scalar
        def _(act):
            act.wait_ge(conv_zeroed, 1)
            for b in range(TB):
                for g in range(CGROUPS):
                    r = S * b + CG * g
                    act.dma_start(conv_f[r:r + CG, :, r:r + CG],
                                  a["conv_w"][CG * g:CG * (g + 1)]).then_inc(conv_loaded, 16)
            act.wait_ge(conv_loaded, 16 * TB * CGROUPS)
            act.activation(conv_w[:, 0], conv_f[:], ACT.Copy).then_inc(conv_hi, 1)
            for n, bias in enumerate((b0, b1)):
                act.wait_ge(hid_psum, n + 1)
                act.activation(hid[:, n], bank[1 + n][:, 0:B], ACT.Gelu, bias=bias[:, 0:1]).then_inc(hid_done, 1)
            act.wait_ge(att_step, 2)
            act.activation(att[:], att[:], ACT.Exp).then_inc(att_exp, 1)

        @block.tensor
        def _(pe):
            pe.wait_ge(params_loaded, 16 * 12)
            pe.matmul(bank[0][:, 0:S], cond_T[:], cw_T[:], start=True, stop=True).then_inc(ctx_psum, 1)
            pe.matmul(bank[1][:, 0:B], w0[:], cond_T[:], start=True, stop=True).then_inc(hid_psum, 1)
            pe.wait_ge(hid_done, 1)
            pe.matmul(bank[2][:, 0:B], w1[:], hid[:, 0], start=True, stop=True).then_inc(hid_psum, 1)
            pe.wait_ge(hid_done, 2)
            pe.matmul(bank[3][:, 0:COND_K], hid[:, 1], w2[:], start=True, stop=True).then_inc(att_psum, 1)
            pe.wait_ge(att_step, 5)
            pe.transpose(bank[4][0:COND_K, 0:B], att[:], ident[:]).then_inc(att_T_psum, 1)
            pe.wait_ge(att_T_done, 1)
            for n in range(2):
                pe.matmul(bank[5 + n][:, :], att_T[:], kern[:, 512 * n:512 * (n + 1)],
                          start=True, stop=True).then_inc(agg_psum, 1)
            pe.matmul(bank[7][:, 0:S], att_T[:], kern_b[:], start=True, stop=True).then_inc(agg_psum, 1)

        @block.vector
        def _(dve):
            dve.wait_ge(ctx_psum, 1)
            dve.tensor_tensor(ctx_sb[:], bank[0][:, 0:S], fside[:], ALU.add).then_inc(ctx_added, 1)
            dve.wait_ge(conv_hi, 1)
            dve.tensor_tensor(conv_w[:, 1], conv_f[:], conv_w[:, 0], ALU.subtract).then_inc(conv_lo, 1)
            dve.wait_ge(att_psum, 1)
            dve.tensor_tensor(att[:], bank[3][:, 0:COND_K], b2[:], ALU.add).then_inc(att_step, 1)
            dve.wait_ge(att_step, 1)
            dve.tensor_reduce(stat[:, 0:1], att[:], AX.X, ALU.max).then_inc(att_max, 1)
            dve.wait_ge(att_max, 1)
            dve.tensor_scalar(att[:], att[:], stat[:, 0:1], None, ALU.subtract).then_inc(att_step, 1)
            dve.wait_ge(att_exp, 1)
            dve.reduce_sum(stat[:, 1:2], att[:], AX.X).then_inc(att_step, 1)
            dve.wait_ge(att_step, 3)
            dve.reciprocal(stat[:, 2:3], stat[:, 1:2]).then_inc(att_step, 1)
            dve.wait_ge(att_step, 4)
            dve.tensor_scalar(att[:], att[:], stat[:, 2:3], None, ALU.mult).then_inc(att_step, 1)
            dve.wait_ge(att_T_psum, 1)
            dve.tensor_copy(att_T[:], bank[4][0:COND_K, 0:B]).then_inc(att_T_done, 1)
            for n in range(2):
                dve.wait_ge(agg_psum, n + 1)
                dve.tensor_copy(aggw_sb[:, 512 * n:512 * (n + 1)], bank[5 + n][:, :]).then_inc(agg_done, 1)
            dve.wait_ge(agg_psum, 3)
            dve.tensor_copy(aggb_sb[:], bank[7][:, 0:S]).then_inc(agg_done, 1)


def conv_and_dequant(nc, a, bank, x1, hT, conv_w, ctx_rows, w_split):
    with ExitStack() as c:
        def sb(name, shape, dt=F32):
            return c.enter_context(nc.sbuf_tensor(name, shape, dt))

        def sem(name):
            return c.enter_context(nc.semaphore(name))

        ctx_bc = sb("ctx_bc", [P, TOKENS])
        x_hl = sb("x_hl", [P, 2, 2, XP], F16)
        h_f = sb("h_f", [P, 2, KT, P])
        codes = sb("codes", [P, 2, WSTEP], I32)
        scales = sb("scales", [P, 2, WSTEP])
        w_f = sb("w_f", [P, 2, WSTEP])
        w_hl = sb("w_hl", [P, 2, 2, WSTEP], F16)

        pads_zeroed = sem("pads_zeroed")
        ctx_loaded = sem("ctx_loaded")
        x_loaded = [sem(f"x_loaded{n}") for n in range(2)]
        codes_loaded = [sem(f"codes_loaded{n}") for n in range(2)]
        w_stored = [sem(f"w_stored{n}") for n in range(2)]
        x_hi = sem("x_hi")
        x_lo = sem("x_lo")
        conv_psum = sem("conv_psum")
        h_added = sem("h_added")
        h_hi = sem("h_hi")
        h_lo = sem("h_lo")
        w_dequant = sem("w_dequant")
        w_hi = sem("w_hi")
        w_lo = sem("w_lo")
        block = c.enter_context(nc.Block())
        ROUNDS = TILES // 2

        x_rows = a["x"].rearrange("(t p) l -> t p l", p=P)

        def x_cols(n):
            return x_hl[:, n, :, PAD:PAD + D]

        @block.sync
        def _(sp):
            def load(t, n):
                sp.dma_start(x1[:, bass.ds(t, 1)], x_rows[bass.ds(t, 1)].rearrange("t p l -> p t l")).then_inc(x_loaded[n], 16)
                sp.dma_start(codes[:, n], a["codes"][bass.ds(t, 1)].rearrange("t p n -> p (t n)")).then_inc(codes_loaded[n], 16)
                sp.dma_start(scales[:, n], a["scales"][bass.ds(t, 1)].rearrange("t n -> (t n)")
                             .partition_broadcast(P)).then_inc(codes_loaded[n], 16)

            def store(t, n):
                sp.wait_ge(w_lo, t + 1)
                sp.dma_start(w_split[:, :, bass.ds(t * WSTEP, WSTEP)], w_hl[:, n]).then_inc(w_stored[n], 16)

            for n in range(2):
                load(n, n)
            sp.dma_start(ctx_bc[:], ctx_rows.rearrange("b s -> (b s)").partition_broadcast(P)).then_inc(ctx_loaded, 16)
            with sp.Fori(0, ROUNDS - 1) as r:
                for n in range(2):
                    store(2 * r + n, n)
                    load(2 * r + n + 2, n)
            for n in range(2):
                store(TILES - 2 + n, n)
            for n in range(2):
                sp.wait_ge(w_stored[n], 16 * ROUNDS)

        @block.scalar
        def _(act):
            def split_x(t, r, n):
                act.wait_ge(x_loaded[n], 16 * (r + 1))
                act.activation(x_hl[:, n, 0, PAD:PAD + D], x1[:, bass.ds(t, 1)].rearrange("p t l -> p (t l)"),
                               ACT.Copy).then_inc(x_hi, 1)

            def rest(t, r, n, first):
                if not first:
                    act.wait_ge(w_stored[n], 16 * r)
                act.wait_ge(w_dequant, t + 1)
                act.activation(w_hl[:, n, 0], w_f[:, n], ACT.Copy, scale=WSCALE).then_inc(w_hi, 1)
                act.wait_ge(h_added, t + 1)
                act.activation(hT[:, :, 0, bass.ds(t * P, P)], h_f[:, n], ACT.Copy).then_inc(h_hi, 1)

            act.wait_ge(pads_zeroed, 1)
            split_x(0, 0, 0)
            split_x(1, 0, 1)
            for n in range(2):
                rest(n, 0, n, True)
                split_x(n + 2, 1, n)
            with act.Fori(1, ROUNDS - 1) as r:
                for n in range(2):
                    rest(2 * r + n, r, n, False)
                    split_x(2 * r + n + 2, r + 1, n)
            for n in range(2):
                rest(TILES - 2 + n, ROUNDS - 1, n, False)

        @block.gpsimd
        def _(pool):
            def split_x(t, n):
                pool.wait_ge(x_hi, t + 1)
                pool.tensor_tensor(x_hl[:, n, 1, PAD:PAD + D], x1[:, bass.ds(t, 1)].rearrange("p t l -> p (t l)"),
                                   x_hl[:, n, 0, PAD:PAD + D], ALU.subtract).then_inc(x_lo, 1)

            def split_h(t, n):
                pool.wait_ge(h_hi, t + 1)
                pool.tensor_tensor(hT[:, :, 1, bass.ds(t * P, P)], h_f[:, n], hT[:, :, 0, bass.ds(t * P, P)],
                                   ALU.subtract).then_inc(h_lo, 1)

            pool.memset(x_hl[:], 0.0).then_inc(pads_zeroed, 1)
            for n in range(2):
                split_x(n, n)
            with pool.Fori(0, ROUNDS - 1) as r:
                for n in range(2):
                    split_h(2 * r + n, n)
                    split_x(2 * r + n + 2, n)
            for n in range(2):
                split_h(TILES - 2 + n, n)

        @block.vector
        def _(dve):
            def work(t, r, n, first):
                dve.wait_ge(codes_loaded[n], 32 * (r + 1))
                dve.scalar_tensor_tensor(out=w_f[:, n], in0=codes[:, n], scalar=-8.0, in1=scales[:, n],
                                         op0=ALU.add, op1=ALU.mult).then_inc(w_dequant, 1)
                dve.wait_ge(w_hi, t + 1)
                dve.scalar_tensor_tensor(out=w_hl[:, n, 1], in0=w_f[:, n], scalar=WSCALE, in1=w_hl[:, n, 0],
                                         op0=ALU.mult, op1=ALU.subtract).then_inc(w_lo, 1)
                dve.wait_ge(conv_psum, t + 1)
                if not first:
                    dve.wait_ge(h_lo, t - 1)
                dve.tensor_tensor(h_f[:, n], bank[n][:].rearrange("p (k t) -> p k t", k=KT),
                                  ctx_bc[:, bass.ds(t * P, P)].unsqueeze(1).broadcast_to([P, KT, P]),
                                  ALU.add).then_inc(h_added, 1)

            dve.wait_ge(ctx_loaded, 16)
            for n in range(2):
                work(n, 0, n, True)
            with dve.Fori(1, ROUNDS) as r:
                for n in range(2):
                    work(2 * r + n, r, n, False)

        @block.tensor
        def _(pe):
            def conv(t, n, first):
                pe.wait_ge(x_lo, t + 1)
                if not first:
                    pe.wait_ge(h_added, t - 1)
                for k in range(KT):
                    for tap in range(TAPS):
                        for xp, wp in PASSES:
                            mm = pe.matmul(bank[n][:, k * P:(k + 1) * P], x_hl[:, n, xp, k * P + tap:k * P + tap + P],
                                           conv_w[:, wp, tap], start=tap == 0 and (xp, wp) == PASSES[0],
                                           stop=tap == TAPS - 1 and (xp, wp) == PASSES[-1])
                mm.then_inc(conv_psum, 1)

            for n in range(2):
                conv(n, n, True)
            with pe.Fori(1, ROUNDS) as r:
                for n in range(2):
                    conv(2 * r + n, n, False)


def attention(nc, c, a, bank, x1, hT, w_split):
    def sb(name, shape, dt=F32):
        return c.enter_context(nc.sbuf_tensor(name, shape, dt))

    def sem(name):
        return c.enter_context(nc.semaphore(name))

    STEPS = NKV * CHUNKS
    w_g = sb("w_g", [P, 2, WG], F16)
    q_hl = sb("q_hl", [P, 2, RF, CHUNK], F16)
    k_hl = sb("k_hl", [P, 2, CHUNK], F16)
    v_hl = sb("v_hl", [P, 2, CT, HD], F16)
    o_hl = sb("o_hl", [P, 2, CT, RF, P], F16)
    pad_hl = sb("pad_hl", [P, 2 * CT * RF, TB, S], F16)
    prod = sb("prod", [P, 2, 2, CHUNK])
    y_hl = sb("y_hl", [P, 2, CHUNK], F16)
    k_prod = sb("k_prod", [P, 2, CHUNK])
    sc = sb("sc", [P, CHUNK])
    ex = sb("ex", [P, CHUNK])
    p_hl = sb("p_hl", [P, 2, CHUNK], F16)
    pT_hl = sb("pT_hl", [P, 2 * CT * RF, S], F16)
    stats = sb("stats", [P, 3, CT * RF])
    cos2 = sb("cos2", [P, S])
    sin2 = sb("sin2", [P, S])
    sin_k = sb("sin_k", [P, S])
    mask_f = sb("mask_f", [P, S])
    ident_f = sb("ident_f", [P, P])
    mask_b = sb("mask_b", [P, CT * RF, S], BF16)
    ident_b = sb("ident_b", [P, P], BF16)

    consts_loaded = sem("consts_loaded")
    consts_ready = sem("consts_ready")
    pad_zeroed = sem("pad_zeroed")
    wqkv_loaded = sem("wqkv_loaded")
    wo_loaded = sem("wo_loaded")
    k_psum = sem("k_psum")
    pair_psum = sem("pair_psum")
    v_psum = sem("v_psum")
    scores_psum = sem("scores_psum")
    pv_psum = sem("pv_psum")
    o_psum = sem("o_psum")
    k_products = sem("k_products")
    k_rotated = sem("k_rotated")
    k_hi = sem("k_hi")
    k_ready = sem("k_ready")
    q_products = sem("q_products")
    q_rotated = sem("q_rotated")
    q_hi = sem("q_hi")
    q_lo = sem("q_lo")
    q_moved = sem("q_moved")
    q_ready = sem("q_ready")
    v_hi = sem("v_hi")
    v_ready = sem("v_ready")
    sc_read = sem("sc_read")
    max_done = sem("max_done")
    shifted = sem("shifted")
    exp_done = sem("exp_done")
    sum_done = sem("sum_done")
    inv_done = sem("inv_done")
    probs = sem("probs")
    probs_hi = sem("probs_hi")
    probs_lo = sem("probs_lo")
    probs_T = sem("probs_T")
    probs_padded = sem("probs_padded")
    out_hi = sem("out_hi")
    out_ready = sem("out_ready")
    block = c.enter_context(nc.Block())

    def w_cols(part, col, n):
        return w_g[:, part, col:col + n]

    def table(t, parts=slice(0, P)):
        n = parts.stop - parts.start
        return t[parts, :].unsqueeze(1).broadcast_to([n, CHUNK // S, S])

    def by_s(ap):
        return ap.rearrange("p (b s) -> p b s", s=S)

    @block.sync
    def _(sp):
        for dst, src in ((cos2, a["cos2"]), (sin2, a["sin2"]), (sin_k, a["sin_k"]), (mask_f, a["mask"]), (ident_f, a["ident"])):
            sp.dma_start(dst[:], src).then_inc(consts_loaded, 16)

        def load_qkv(g):
            sp.dma_start(w_g[:, :, 0:WO], w_split[:, :, bass.ds(g * WG, WO)]).then_inc(wqkv_loaded, 16)

        def load_o(g):
            sp.dma_start(w_g[:, :, WO:WG], w_split[:, :, bass.ds(g * WG + WO, WG - WO)]).then_inc(wo_loaded, 16)

        load_qkv(0)
        load_o(0)
        with sp.Fori(1, NKV) as g:
            sp.wait_ge(v_psum, CHUNKS * g)
            load_qkv(g)
            sp.wait_ge(o_psum, CT * CHUNKS * g)
            load_o(g)

    @block.tensor
    def _(pe):
        def head_of(n):
            return n // CHUNKS if isinstance(n, int) else n >> 3

        def tok(n):
            return n % CHUNKS * CHUNK if isinstance(n, int) else (n & (CHUNKS - 1)) * CHUNK

        def project(n, after=None):
            t0 = tok(n)
            pe.wait_ge(wqkv_loaded, 16 * (head_of(n) + 1))
            i = 0
            for kt in range(KT):
                for wp, hp in PASSES:
                    mm = pe.matmul(bank[4][:], w_cols(wp, WK + kt * HD, HD), hT[:, kt, hp, bass.ds(t0, CHUNK)],
                                   start=i == 0, stop=i == 3 * KT - 1)
                    i += 1
            mm.then_inc(k_psum, 1)
            if after is not None:
                pe.wait_ge(sc_read, after + 1)
            for pair in range(2):
                for eo in range(2):
                    i = 0
                    for kt in range(KT):
                        for wp, hp in PASSES:
                            mm = pe.matmul(bank[2 * pair + eo][:], w_cols(wp, WQ + kt * 512 + (2 * pair + eo) * P, P),
                                           hT[:, kt, hp, bass.ds(t0, CHUNK)], start=i == 0, stop=i == 3 * KT - 1)
                            i += 1
                mm.then_inc(pair_psum, 1)

        def project_v(n):
            t0 = tok(n)
            pe.wait_ge(q_products, 4 * n + 2)
            for j in range(CT):
                i = 0
                for kt in range(KT):
                    for hp, wp in PASSES:
                        mm = pe.matmul(bank[0][:, j * HD:(j + 1) * HD], hT[:, kt, hp, bass.ds(t0 + j * P, P)],
                                       w_cols(wp, WV + kt * HD, HD), start=i == 0, stop=i == 3 * KT - 1)
                        i += 1
            mm.then_inc(v_psum, 1)

        def scores(i):
            pe.wait_ge(k_ready, i + 1)
            pe.wait_ge(q_ready, 2 * i + 2)
            pe.matmul(bank[1][:], ident_b[:], mask_b[:].rearrange("p n s -> p (n s)"), start=True, stop=False,
                      skip_group_check=True)
            for j in range(CT):
                for kp, qp in PASSES:
                    for b in range(TB):
                        t = j * P + b * S
                        mm = pe.matmul(bank[1][b * S:(b + 1) * S, j * P:(j + 1) * P], k_hl[:, kp, t:t + S],
                                       q_hl[:, qp, :, t:t + S], start=False, stop=(kp, qp) == PASSES[-1] and j == CT - 1,
                                       skip_group_check=True)
            mm.then_inc(scores_psum, 1)

        def values(i):
            pe.wait_ge(probs_padded, i + 1)
            pe.wait_ge(v_ready, i + 1)
            for j in range(CT):
                for n, (vp, pp) in enumerate(PASSES):
                    mm = pe.matmul(bank[4 + j][:], v_hl[:, vp, j],
                                   pad_hl[:, (pp * CT + j) * RF:(pp * CT + j + 1) * RF].rearrange("p n b s -> p (n b s)"),
                                   start=n == 0, stop=n == 2)
                mm.then_inc(pv_psum, 1)

        def output(i):
            pe.wait_ge(wo_loaded, 16 * (head_of(i) + 1))
            for j in range(CT):
                pe.wait_ge(out_ready, CT * i + j + 1)
                n = 0
                for h in range(RF):
                    for op, wp in PASSES:
                        mm = pe.matmul(bank[4 + j][:], o_hl[:, op, j, h], w_o(wp, h), start=n == 0, stop=n == 3 * RF - 1)
                        n += 1
                mm.then_inc(o_psum, 1)

        def w_o(part, h):
            return w_cols(part, WO + h * D, D)

        pe.wait_ge(consts_ready, 2)
        project(0)
        project_v(0)
        with pe.Fori(0, STEPS - 1) as i:
            scores(i)
            project(i + 1, after=i)
            values(i)
            project_v(i + 1)
            output(i)
        scores(STEPS - 1)
        values(STEPS - 1)
        output(STEPS - 1)

    @block.vector
    def _(dve):
        def rotate_k(n):
            dve.wait_ge(k_psum, n + 1)
            dve.tensor_tensor(by_s(k_prod[:, 0]), by_s(bank[4][:]), table(cos2), ALU.mult)
            for h in range(2):
                src = slice(64 * (1 - h), 64 * (2 - h))
                ins = dve.tensor_tensor(by_s(k_prod[64 * h:64 * (h + 1), 1]), by_s(bank[4][src, :]), table(sin_k, src), ALU.mult)
            ins.then_inc(k_products, 1)

        def rotate_q(n, pair):
            dve.wait_ge(pair_psum, 2 * n + pair + 1)
            for eo in range(2):
                if pair == 1:
                    dve.wait_ge(q_lo, 4 * n + eo + 1)
                dve.tensor_tensor(by_s(prod[:, eo, 0]), by_s(bank[2 * pair + eo][:]), table(cos2), ALU.mult)
                dve.tensor_tensor(by_s(prod[:, eo, 1]), by_s(bank[2 * pair + 1 - eo][:]), table(sin2), ALU.mult).then_inc(q_products, 1)

        def gather_q(n, pair):
            even, odd = 2 * pair, 2 * pair + 1
            dve.wait_ge(q_lo, 4 * n + 2 * pair + 2)
            dve.tensor_copy(q_hl[0:64, :, odd], q_hl[64:128, :, even]).then_inc(q_moved, 1)
            dve.tensor_copy(q_hl[64:128, :, odd], y_hl[64:128])
            dve.wait_ge(q_moved, 2 * n + pair + 1)
            dve.tensor_copy(q_hl[64:128, :, even], y_hl[0:64]).then_inc(q_ready, 1)

        def finish_v(n):
            dve.wait_ge(v_hi, n + 1)
            dve.scalar_tensor_tensor(out=v_hl[:, 1].rearrange("p j d -> p (j d)"), in0=bank[0][:], scalar=1 / WSCALE,
                                     in1=v_hl[:, 0].rearrange("p j d -> p (j d)"), op0=ALU.mult,
                                     op1=ALU.subtract).then_inc(v_ready, 1)

        def softmax_exp(i):
            dve.wait_ge(scores_psum, i + 1)
            dve.transpose(sc[:], bank[1][:]).then_inc(sc_read, 1)
            dve.wait_ge(sc_read, i + 1)
            dve.tensor_reduce(stats[:, 0], by_s(sc[:]), AX.X, ALU.max).then_inc(max_done, 1)
            dve.wait_ge(max_done, i + 1)
            dve.tensor_tensor(by_s(sc[:]), by_s(sc[:]), stats[:, 0].unsqueeze(2).broadcast_to([P, CT * RF, S]),
                              ALU.subtract).then_inc(shifted, 1)

        def softmax_norm(i):
            dve.wait_ge(exp_done, i + 1)
            dve.reduce_sum(stats[:, 1], by_s(ex[:]), AX.X).then_inc(sum_done, 1)
            dve.wait_ge(sum_done, i + 1)
            dve.reciprocal(stats[:, 2], stats[:, 1]).then_inc(inv_done, 1)
            dve.wait_ge(inv_done, i + 1)
            dve.tensor_tensor(by_s(ex[:]), by_s(ex[:]), stats[:, 2].unsqueeze(2).broadcast_to([P, CT * RF, S]),
                              ALU.mult).then_inc(probs, 1)

        def softmax_pad(i):
            dve.wait_ge(probs_lo, i + 1)
            dve.transpose(pT_hl[:].rearrange("p n s -> p (n s)"), p_hl[:].rearrange("p h n -> p (h n)")).then_inc(probs_T, 1)
            dve.wait_ge(probs_T, i + 1)
            for b in range(TB):
                ins = dve.tensor_copy(pad_hl[b * S:(b + 1) * S, :, b], pT_hl[b * S:(b + 1) * S])
            ins.then_inc(probs_padded, 1)

        def finish_out(i):
            for j in range(CT):
                dve.wait_ge(out_hi, CT * i + j + 1)
                dve.tensor_tensor(o_hl[:, 1, j].rearrange("p h t -> p (h t)"), bank[4 + j][:],
                                  o_hl[:, 0, j].rearrange("p h t -> p (h t)"), ALU.subtract).then_inc(out_ready, 1)

        def add_out(i, tiles=range(CT)):
            for j in tiles:
                if isinstance(i, int):
                    tile = i % CHUNKS * CT + j
                else:
                    tile = (i & (CHUNKS - 1)) * CT + j
                dst = x1[:, bass.ds(tile, 1)].rearrange("p t l -> p (t l)")
                dve.wait_ge(o_psum, CT * i + j + 1)
                dve.scalar_tensor_tensor(out=dst, in0=bank[4 + j][:], scalar=1 / WSCALE, in1=dst,
                                         op0=ALU.mult, op1=ALU.add)

        dve.wait_ge(consts_loaded, 80)
        dve.tensor_copy(mask_b[:], mask_f[:].unsqueeze(1).broadcast_to([P, CT * RF, S])).then_inc(consts_ready, 1)
        dve.tensor_copy(ident_b[:], ident_f[:]).then_inc(consts_ready, 1)
        rotate_k(0)
        rotate_q(0, 0)
        gather_q(0, 0)
        rotate_q(0, 1)
        gather_q(0, 1)
        finish_v(0)
        dve.wait_ge(pad_zeroed, 1)
        with dve.Fori(0, STEPS - 1) as i:
            softmax_exp(i)
            rotate_k(i + 1)
            softmax_norm(i)
            rotate_q(i + 1, 0)
            softmax_pad(i)
            gather_q(i + 1, 0)
            finish_out(i)
            rotate_q(i + 1, 1)
            finish_v(i + 1)
            add_out(i, range(1))
            gather_q(i + 1, 1)
            add_out(i, range(1, CT))
        softmax_exp(STEPS - 1)
        softmax_norm(STEPS - 1)
        softmax_pad(STEPS - 1)
        finish_out(STEPS - 1)
        add_out(STEPS - 1)

    @block.gpsimd
    def _(pool):
        def rotate_k(n):
            pool.wait_ge(k_products, n + 1)
            pool.tensor_tensor(k_prod[:, 0], k_prod[:, 0], k_prod[:, 1], ALU.add).then_inc(k_rotated, 1)

        def finish_k(n):
            pool.wait_ge(k_hi, n + 1)
            pool.tensor_tensor(k_hl[:, 1], k_prod[:, 0], k_hl[:, 0], ALU.subtract).then_inc(k_ready, 1)

        def rotate_q(n, pair):
            for eo in range(2):
                stage = 2 * pair + eo
                pool.wait_ge(q_products, 4 * n + stage + 1)
                pool.tensor_tensor(prod[:, eo, 0], prod[:, eo, 0], prod[:, eo, 1],
                                   ALU.add if eo else ALU.subtract).then_inc(q_rotated, 1)
                dst = y_hl if eo else q_hl[:, :, 2 * pair]
                pool.wait_ge(q_hi, 4 * n + stage + 1)
                pool.tensor_tensor(dst[:, 1], prod[:, eo, 0], dst[:, 0], ALU.subtract).then_inc(q_lo, 1)

        def probs_low(i):
            pool.wait_ge(probs_hi, i + 1)
            pool.tensor_tensor(p_hl[:, 1], ex[:], p_hl[:, 0], ALU.subtract).then_inc(probs_lo, 1)

        pool.memset(pad_hl[:], 0.0).then_inc(pad_zeroed, 1)
        rotate_k(0)
        finish_k(0)
        rotate_q(0, 0)
        rotate_q(0, 1)
        with pool.Fori(0, STEPS - 1) as i:
            rotate_k(i + 1)
            finish_k(i + 1)
            probs_low(i)
            rotate_q(i + 1, 0)
            rotate_q(i + 1, 1)
        probs_low(STEPS - 1)

    @block.scalar
    def _(act):
        def exp(i):
            act.wait_ge(shifted, i + 1)
            act.activation(ex[:], sc[:], ACT.Exp, scale=SM_SCALE).then_inc(exp_done, 1)

        def k_high(n):
            act.wait_ge(k_rotated, n + 1)
            act.activation(k_hl[:, 0], k_prod[:, 0], ACT.Copy).then_inc(k_hi, 1)

        def probs_high(i):
            act.wait_ge(probs, i + 1)
            act.activation(p_hl[:, 0], ex[:], ACT.Copy).then_inc(probs_hi, 1)

        def q_high(n, pair):
            for eo in range(2):
                act.wait_ge(q_rotated, 4 * n + 2 * pair + eo + 1)
                if eo == 1 and pair == 1:
                    act.wait_ge(q_ready, 2 * n + 1)
                dst = y_hl if eo else q_hl[:, :, 2 * pair]
                act.activation(dst[:, 0], prod[:, eo, 0], ACT.Copy).then_inc(q_hi, 1)

        def v_high(n):
            act.wait_ge(v_psum, n + 1)
            act.activation(v_hl[:, 0].rearrange("p j d -> p (j d)"), bank[0][:], ACT.Copy, scale=1 / WSCALE).then_inc(v_hi, 1)

        def out_high(i):
            for j in range(CT):
                act.wait_ge(pv_psum, CT * i + j + 1)
                act.activation(o_hl[:, 0, j].rearrange("p h t -> p (h t)"), bank[4 + j][:], ACT.Copy).then_inc(out_hi, 1)

        k_high(0)
        q_high(0, 0)
        q_high(0, 1)
        v_high(0)
        with act.Fori(0, STEPS - 1) as i:
            exp(i)
            k_high(i + 1)
            probs_high(i)
            q_high(i + 1, 0)
            out_high(i)
            v_high(i + 1)
            q_high(i + 1, 1)
        exp(STEPS - 1)
        probs_high(STEPS - 1)
        out_high(STEPS - 1)


def mix_and_ffn(nc, c, a, bank, x1, aggb_rows, aggw_rows, out):
    def sb(name, shape, dt=F32):
        return c.enter_context(nc.sbuf_tensor(name, shape, dt))

    def sem(name):
        return c.enter_context(nc.semaphore(name))

    mixw_f = sb("mixw_f", [P, TILES, P])
    mixw = sb("mixw", [P, 2, TILES, P], F16)
    aggb = sb("aggb", [P, TOKENS])
    base_f = sb("base_f", [P, KT, D])
    base = sb("base", [P, 2, KT, D], F16)
    gl_f = sb("gl_f", [P, KT, GL])
    gl = sb("gl", [P, 2, KT, GL], F16)
    lb_f = sb("lb_f", [EH, 2, D])
    lb = sb("lb", [EH, 2, 2, D], F16)
    ident = sb("ident_m", [P, P])
    iota = sb("iota", [P, EXPERTS])
    x_hl = sb("xm_hl", [P, 2, 2, D], F16)
    y_f = sb("y_f", [P, 2, D])
    y_hl = sb("ym_hl", [P, 2, 2, D], F16)
    logits = sb("logits", [P, 2, EXPERTS])
    top = sb("top", [P, 2, 8])
    top_at = sb("top_at", [P, 2, 8], U32)
    topv = sb("topv", [P, 2, 8])
    gates = sb("gates", [P, 2, 2, EXPERTS])
    lora = sb("lora", [P, 2, ER])
    loraT = sb("loraT", [EH, 2, 2, 2, P], F16)
    res = sb("res", [P, 2, D])

    mixw_zeroed = sem("mixw_zeroed")
    mixw_loaded = sem("mixw_loaded")
    w_loaded = sem("w_loaded")
    w_his = sem("w_his")
    w_ready = sem("w_ready")
    xs_hi = sem("xs_hi")
    xs_ready = sem("xs_ready")
    y_psum = sem("y_psum")
    y_added = sem("y_added")
    y_hi = sem("y_hi")
    y_ready = sem("y_ready")
    gl_psum = sem("gl_psum")
    base_psum = sem("base_psum")
    gate_step = sem("gate_step")
    gate_exp = sem("gate_exp")
    lora_gated = sem("lora_gated")
    loraT_psum = sem("loraT_psum")
    loraT_hi = sem("loraT_hi")
    loraT_ready = sem("loraT_ready")
    ffn_psum = sem("ffn_psum")
    res_done = sem("res_done")
    out_stored = [sem(f"out_stored{n}") for n in range(2)]
    block = c.enter_context(nc.Block())
    ROUNDS = TILES // 2
    GATE_STEPS = 9
    out_rows = out.rearrange("(t p) l -> t p l", p=P)

    def tile_of(t):
        return x1[:, bass.ds(t, 1)].rearrange("p t l -> p (t l)")

    splits = ((base, base_f, FSCALE), (gl, gl_f, FSCALE), (lb, lb_f, FSCALE), (mixw, mixw_f, FSCALE))

    @block.sync
    def _(sp):
        for dst, src in ((base_f, a["base_T"]), (gl_f, a["gl_T"]), (lb_f, a["lb_T"]), (ident, a["ident"]),
                         (iota, a["iota"].partition_broadcast(P))):
            sp.dma_start(dst[:], src).then_inc(w_loaded, 16)
        sp.dma_start(aggb[:], aggb_rows.rearrange("b s -> (b s)").partition_broadcast(P)).then_inc(w_loaded, 16)
        sp.wait_ge(mixw_zeroed, 1)
        for b in range(TB):
            sp.dma_start(mixw_f[b * S:(b + 1) * S, :, b * S:(b + 1) * S],
                         aggw_rows.rearrange("(t b) (i o) -> b i t o", b=TB, i=S)[b]).then_inc(mixw_loaded, 16)
        with sp.Fori(0, ROUNDS) as r:
            for n in range(2):
                t = 2 * r + n
                sp.wait_ge(res_done, t + 1)
                sp.dma_start(out_rows[bass.ds(t, 1)].rearrange("t p l -> p (t l)"), res[:, n]).then_inc(out_stored[n], 16)
        for n in range(2):
            sp.wait_ge(out_stored[n], 16 * ROUNDS)

    @block.tensor
    def _(pe):
        def mix(t, n):
            pe.wait_ge(xs_ready, t + 1)
            for k in range(KT):
                for i, (xp, wp) in enumerate(PASSES):
                    mm = pe.matmul(bank[n][:, k * P:(k + 1) * P], x_hl[:, n, xp, k * P:(k + 1) * P],
                                   mixw[:, wp, bass.ds(t, 1)].rearrange("p t o -> p (t o)"), start=i == 0, stop=i == 2)
            mm.then_inc(y_psum, 1)

        def gate_lora(t, n):
            pe.wait_ge(y_ready, t + 1)
            i = 0
            for k in range(KT):
                for yp, wp in PASSES:
                    mm = pe.matmul(bank[4 + n][:, 0:GL], y_hl[:, n, yp, k * P:(k + 1) * P], gl[:, wp, k],
                                   start=i == 0, stop=i == 3 * KT - 1)
                    i += 1
            mm.then_inc(gl_psum, 1)

        def base_out(t, n, first):
            if not first:
                pe.wait_ge(res_done, t - 1)
            i = 0
            for k in range(KT):
                for yp, wp in PASSES:
                    pe.matmul(bank[2 + n][:], y_hl[:, n, yp, k * P:(k + 1) * P], base[:, wp, k],
                              start=i == 0, stop=False, skip_group_check=True)
                    i += 1

        def lora_out(t, n):
            pe.wait_ge(lora_gated, t + 1)
            for h in range(2):
                mm = pe.transpose(bank[6 + n][0:EH, h * P:(h + 1) * P], lora[:, n, h * EH:(h + 1) * EH], ident[:])
            mm.then_inc(loraT_psum, 1)
            pe.wait_ge(loraT_ready, t + 1)
            for h in range(2):
                for i, (lp, wp) in enumerate(PASSES):
                    mm = pe.matmul(bank[2 + n][:], loraT[:, n, lp, h], lb[:, wp, h], start=False,
                                   stop=h == 1 and i == 2, skip_group_check=True)
            mm.then_inc(ffn_psum, 1)

        def body(t, n, first, last):
            gate_lora(t, n)
            if not last:
                mix(t + 1, 1 - n)
            base_out(t, n, first)
            lora_out(t, n)

        pe.wait_ge(w_ready, len(splits))
        mix(0, 0)
        for n in range(2):
            body(n, n, True, False)
        with pe.Fori(1, ROUNDS - 1) as r:
            for n in range(2):
                body(2 * r + n, n, False, False)
        for n in range(2):
            body(TILES - 2 + n, n, False, n == 1)

    @block.scalar
    def _(act):
        def x_high(t, n):
            act.activation(x_hl[:, n, 0], tile_of(t), ACT.Copy).then_inc(xs_hi, 1)

        def y_high(t, n):
            act.wait_ge(y_added, t + 1)
            act.activation(y_hl[:, n, 0], y_f[:, n], ACT.Copy).then_inc(y_hi, 1)

        def exp(t, n):
            act.wait_ge(gate_step, GATE_STEPS * t + 3)
            act.activation(topv[:, n, 3:4], topv[:, n, 2:3], ACT.Exp).then_inc(gate_exp, 1)

        def lora_high(t, n):
            act.wait_ge(loraT_psum, t + 1)
            act.activation(loraT[:, n, 0], bank[6 + n][0:EH, 0:2 * P].rearrange("p (h t) -> p h t", h=2),
                           ACT.Copy).then_inc(loraT_hi, 1)

        act.wait_ge(w_loaded, 16 * 6)
        for dst, src, scale in splits:
            if src is mixw_f:
                act.wait_ge(mixw_loaded, 16 * TB)
            act.activation(dst[:, 0], src[:], ACT.Copy, scale=scale).then_inc(w_his, 1)
        x_high(0, 0)
        x_high(1, 1)
        y_high(0, 0)
        with act.Fori(0, ROUNDS - 1) as r:
            for n in range(2):
                x_high(2 * r + n + 2, n)
                exp(2 * r + n, n)
                y_high(2 * r + n + 1, 1 - n)
                lora_high(2 * r + n, n)
        exp(TILES - 2, 0)
        y_high(TILES - 1, 1)
        lora_high(TILES - 2, 0)
        exp(TILES - 1, 1)
        lora_high(TILES - 1, 1)

    @block.gpsimd
    def _(pool):
        def x_low(t, n):
            pool.wait_ge(xs_hi, t + 1)
            pool.tensor_tensor(x_hl[:, n, 1], tile_of(t), x_hl[:, n, 0], ALU.subtract).then_inc(xs_ready, 1)

        def y_low(t, n):
            pool.wait_ge(y_hi, t + 1)
            pool.tensor_tensor(y_hl[:, n, 1], y_f[:, n], y_hl[:, n, 0], ALU.subtract).then_inc(y_ready, 1)

        pool.memset(mixw_f[:], 0.0).then_inc(mixw_zeroed, 1)
        x_low(0, 0)
        x_low(1, 1)
        y_low(0, 0)
        with pool.Fori(0, ROUNDS - 1) as r:
            for n in range(2):
                x_low(2 * r + n + 2, n)
                y_low(2 * r + n + 1, 1 - n)
        y_low(TILES - 1, 1)

    @block.vector
    def _(dve):
        def add_bias(t, n):
            dve.wait_ge(y_psum, t + 1)
            dve.scalar_tensor_tensor(out=y_f[:, n].rearrange("p (k t) -> p k t", k=KT),
                                     in0=bank[n][:].rearrange("p (k t) -> p k t", k=KT), scalar=1 / FSCALE,
                                     in1=aggb[:, bass.ds(t * P, P)].unsqueeze(1).broadcast_to([P, KT, P]),
                                     op0=ALU.mult, op1=ALU.add).then_inc(y_added, 1)

        def gate(t, n):
            count = [0]

            def step(ins):
                count[0] += 1
                ins.then_inc(gate_step, 1)
                dve.wait_ge(gate_step, GATE_STEPS * t + count[0])

            v = topv[:, n]
            dve.wait_ge(gl_psum, t + 1)
            step(dve.tensor_scalar(logits[:, n], bank[4 + n][:, 0:EXPERTS], 1 / FSCALE, None, ALU.mult))
            dve.memset(v[:, 7:8], 0.0)
            step(dve.max(top[:, n], logits[:, n]))
            step(dve.tensor_tensor(v[:, 2:3], top[:, n, 1:2], top[:, n, 0:1], ALU.subtract))
            dve.memset(v[:, 7:8], 0.0)
            step(dve.max_index(top_at[:, n], top[:, n], logits[:, n]))
            dve.tensor_copy(v[:, 0:2], top_at[:, n, 0:2])
            dve.wait_ge(gate_exp, t + 1)
            step(dve.tensor_scalar(v[:, 4:5], v[:, 3:4], 1.0, None, ALU.add))
            step(dve.reciprocal(v[:, 5:6], v[:, 4:5]))
            step(dve.tensor_tensor(v[:, 6:7], v[:, 3:4], v[:, 5:6], ALU.mult))
            dve.tensor_scalar(gates[:, n, 0], iota[:], v[:, 0:1], v[:, 5:6], ALU.is_equal, ALU.mult)
            step(dve.tensor_scalar(gates[:, n, 1], iota[:], v[:, 1:2], v[:, 6:7], ALU.is_equal, ALU.mult))
            step(dve.tensor_tensor(gates[:, n, 0], gates[:, n, 0], gates[:, n, 1], ALU.add))
            assert count[0] == GATE_STEPS
            dve.scalar_tensor_tensor(out=lora[:, n].rearrange("p (e r) -> p e r", r=RANK),
                                     in0=bank[4 + n][:, EXPERTS:GL].rearrange("p (e r) -> p e r", r=RANK),
                                     scalar=LORA / FSCALE, in1=gates[:, n, 0].unsqueeze(2).broadcast_to([P, EXPERTS, RANK]),
                                     op0=ALU.mult, op1=ALU.mult).then_inc(lora_gated, 1)

        def lora_low(t, n):
            dve.wait_ge(loraT_hi, t + 1)
            dve.tensor_tensor(loraT[:, n, 1], bank[6 + n][0:EH, 0:2 * P].rearrange("p (h t) -> p h t", h=2),
                              loraT[:, n, 0], ALU.subtract).then_inc(loraT_ready, 1)

        def finish(t, r, n, first):
            dve.wait_ge(ffn_psum, t + 1)
            if not first:
                dve.wait_ge(out_stored[n], 16 * r)
            dve.scalar_tensor_tensor(out=res[:, n], in0=bank[2 + n][:], scalar=1 / FSCALE, in1=tile_of(t),
                                     op0=ALU.mult, op1=ALU.add).then_inc(res_done, 1)

        def body(t, r, n, first, last):
            gate(t, n)
            if not last:
                add_bias(t + 1, 1 - n)
            lora_low(t, n)
            finish(t, r, n, first)

        for k, (dst, src, scale) in enumerate(splits):
            dve.wait_ge(w_his, k + 1)
            dve.scalar_tensor_tensor(out=dst[:, 1], in0=src[:], scalar=scale, in1=dst[:, 0], op0=ALU.mult,
                                     op1=ALU.subtract).then_inc(w_ready, 1)
        add_bias(0, 0)
        for n in range(2):
            body(n, 0, n, True, False)
        with dve.Fori(1, ROUNDS - 1) as r:
            for n in range(2):
                body(2 * r + n, r, n, False, False)
        for n in range(2):
            body(TILES - 2 + n, ROUNDS - 1, n, False, n == 1)


def kernel(**inputs):
    import numpy as np
    import concourse.bacc as bacc
    from concourse.bass_utils import run_bass_kernel_spmd

    i = {k: np.asarray(v) for k, v in inputs.items()}

    def cols(codes, perm=None):
        n = codes.shape[1] // NKV
        return codes.reshape(KT, P, NKV, n).transpose(2, 1, 0, 3).reshape(NKV, P, KT * n)

    def split_dims(m, heads):
        rows = m.shape[0]
        if heads == NKV:
            return m.reshape(rows, NKV, HD // 2, 2).transpose(0, 1, 3, 2).reshape(rows, -1)
        return m.reshape(rows, NKV * 2, 2, HD // 2, 2).transpose(0, 1, 4, 2, 3).reshape(rows, -1)

    def by_step(q, k, v, o):
        w = np.concatenate([q, k, v, o], axis=2)
        rows = w.shape[1]
        return np.ascontiguousarray(w.reshape(NKV, rows, STEPS_G, WSTEP).transpose(0, 2, 1, 3).reshape(TILES, rows, WSTEP))

    codes = by_step(cols(split_dims(i["L0_attn_q_codes"], 32)), cols(split_dims(i["L0_attn_k_codes"], NKV)),
                    cols(i["L0_attn_v_codes"]),
                    i["L0_attn_o_codes"].reshape(NKV, RF, P, D).transpose(0, 2, 1, 3).reshape(NKV, P, RF * D))

    def srow(s):
        n = s.shape[1] // NKV
        return s.reshape(KT, NKV, n).transpose(1, 0, 2).reshape(NKV, 1, KT * n)

    scales = by_step(srow(split_dims(i["L0_attn_q_scales"], 32)), srow(split_dims(i["L0_attn_k_scales"], NKV)),
                     srow(i["L0_attn_v_scales"]), i["L0_attn_o_scales"].reshape(NKV, 1, RF * D))[:, 0]

    inv_freq = (1.0 / np.float32(10000.0) ** (np.arange(0, HD, 2, dtype=np.float32) / np.float32(HD))).astype(np.float32)
    f = np.arange(S, dtype=np.float32)[None, :] * inv_freq[:, None]
    cos, sin = np.cos(f) / np.float32(WSCALE), np.sin(f) / np.float32(WSCALE)
    t, s = np.arange(S)[:, None], np.arange(S)[None, :]
    arrays = {
        "x": i["x"].reshape(TOKENS, D),
        "conv_w": i["L0_cond_weight"].reshape(CGROUPS, CG, CG, TAPS).transpose(0, 2, 3, 1).reshape(S, TAPS, CG),
        "cond_T": i["cond_128"].T,
        "cw_T": i["L0_cond_c_weight"].T,
        "fside": i["fside_S_0"],
        "w0": i["L0_cond2_W0"], "w1": i["L0_cond2_W1"], "w2": i["L0_cond2_W2"],
        "b0": i["L0_cond2_b0"].reshape(P, 1), "b1": i["L0_cond2_b1"].reshape(P, 1), "b2": i["L0_cond2_b2"],
        "kern": i["L0_cond2_weight"].reshape(COND_K, S, S).transpose(0, 2, 1).reshape(COND_K, S * S),
        "kern_b": i["L0_cond2_bias_k"],
        "codes": codes,
        "scales": scales,
        "base_T": i["L0_ffn_base_W"].T.reshape(KT, P, D).transpose(1, 0, 2),
        "gl_T": np.concatenate([i["L0_ffn_gate_W"].T, i["L0_ffn_lora_A"].reshape(ER, D).T], axis=1)
        .reshape(KT, P, GL).transpose(1, 0, 2),
        "lb_T": i["L0_ffn_lora_B"].transpose(0, 2, 1).reshape(2, EH, D).transpose(1, 0, 2),
        "ident": np.eye(P, dtype=np.float32),
        "iota": np.arange(EXPERTS, dtype=np.float32),
        "cos2": np.concatenate([cos, cos]),
        "sin2": np.concatenate([sin, sin]),
        "sin_k": np.concatenate([sin, -sin]),
        "mask": np.tile(np.where(t > s, np.float32(-1e30), np.float32(0)), (TB, 1)),
    }
    arrays = {k: np.ascontiguousarray(v) for k, v in arrays.items()}
    nc = bacc.Bacc("TRN2", target_bir_lowering=False, num_devices=1)
    aps = {k: nc.dram_tensor(f"in_{k}", v.shape, mybir.dt.from_np(v.dtype), kind="ExternalInput").ap()
           for k, v in arrays.items()}
    out = nc.dram_tensor("out", [TOKENS, D], F32, kind="ExternalOutput").ap()
    layer(nc, aps, out)
    r = run_bass_kernel_spmd(nc, [{f"in_{k}": v for k, v in arrays.items()}], core_ids=[0])
    return r.results[0]["out"].reshape(B, S, D)
```

```python
from contextlib import ExitStack

import concourse.bass as bass
from concourse import mybir

F32 = mybir.dt.float32
F16 = mybir.dt.float16
BF16 = mybir.dt.bfloat16
I32 = mybir.dt.int32
U32 = mybir.dt.uint32
ALU = mybir.AluOpType
ACT = mybir.ActivationFunctionType
AX = mybir.AxisListType

P = 128
B, S, D = 128, 32, 512
TOKENS = B * S
TILES = TOKENS // P
TB = P // S
KT = D // P
CHUNK = 512
CHUNKS = TOKENS // CHUNK
CT = CHUNK // P
NKV, RF, HD = 8, 4, 128
TAPS, PAD, CGROUPS = 9, 4, 4
CG = S // CGROUPS
XP = D + 2 * PAD
WQ = 2048
WK, WV, WO, WKVO = 0, 512, 1024, 3072
QSTEP = WQ * NKV // TILES
WSTEP = WKVO * NKV // TILES
STEPS_G = TILES // NKV
WSCALE = 256.0
FSCALE = 64.0
SM_SCALE = float(HD) ** -0.5
EXPERTS, RANK, LORA = 28, 8, 2.0
ER = EXPERTS * RANK
EH = ER // 2
GL = EXPERTS + ER
COND_K = 8
PASSES = ((0, 0), (0, 1), (1, 0))


def layer(nc, a, out):
    w_codes = nc.dram_tensor("w_codes", [P, NKV * WQ], F16, kind="Internal").ap()
    w_split = nc.dram_tensor("w_split", [P, 2, NKV * WKVO], F16, kind="Internal").ap()
    ctx_rows = nc.dram_tensor("ctx_rows", [B, S], F32, kind="Internal").ap()
    aggb_rows = nc.dram_tensor("aggb_rows", [B, S], F32, kind="Internal").ap()
    aggw_rows = nc.dram_tensor("aggw_rows", [B, S * S], F32, kind="Internal").ap()
    with ExitStack() as ctx:
        bank = [ctx.enter_context(nc.psum_tensor(f"bank{n}", [P, 512], F32)) for n in range(8)]
        x1 = ctx.enter_context(nc.sbuf_tensor("x1", [P, TILES, D], F32))
        h_ctx = ExitStack()
        hT = h_ctx.enter_context(nc.sbuf_tensor("hT", [P, KT, 2, TOKENS], F16))
        with ExitStack() as c1:
            conv_w = c1.enter_context(nc.sbuf_tensor("conv_w", [P, 2, TAPS, P], F16))
            setup(nc, a, bank, conv_w, ctx_rows, aggb_rows, aggw_rows)
            conv_and_dequant(nc, a, bank, x1, hT, conv_w, ctx_rows, w_codes, w_split)
        with ExitStack() as c2:
            attention(nc, c2, a, bank, x1, hT, w_codes, w_split)
        h_ctx.close()
        with ExitStack() as c3:
            mix_and_ffn(nc, c3, a, bank, x1, aggb_rows, aggw_rows, out)


def setup(nc, a, bank, conv_w, ctx_rows, aggb_rows, aggw_rows):
    with ExitStack() as c:
        def sb(name, shape, dt=F32):
            return c.enter_context(nc.sbuf_tensor(name, shape, dt))

        def sem(name):
            return c.enter_context(nc.semaphore(name))

        conv_f = sb("conv_f", [P, TAPS, P])
        cond_T = sb("cond_T", [P, B])
        cw_T = sb("cw_T", [P, S])
        fside = sb("fside", [P, S])
        w0 = sb("w0", [P, P])
        w1 = sb("w1", [P, P])
        w2 = sb("w2", [P, COND_K])
        b0 = sb("b0", [P, 1])
        b1 = sb("b1", [P, 1])
        b2 = sb("b2", [P, COND_K])
        kern = sb("kern", [COND_K, S * S])
        kern_b = sb("kern_b", [COND_K, S])
        ident = sb("ident_s", [P, P])
        ctx_sb = sb("ctx_sb", [P, S])
        hid = sb("hid", [P, 2, B])
        att = sb("att", [P, COND_K])
        att_T = sb("att_T", [COND_K, B])
        stat = sb("stat", [P, 4])
        aggw_sb = sb("aggw_sb", [P, S * S])
        aggb_sb = sb("aggb_sb", [P, S])

        conv_zeroed = sem("conv_zeroed")
        conv_loaded = sem("conv_loaded")
        params_loaded = sem("params_loaded")
        conv_hi = sem("conv_hi")
        conv_lo = sem("conv_lo")
        ctx_psum = sem("ctx_psum")
        ctx_added = sem("ctx_added")
        hid_psum = sem("hid_psum")
        att_max = sem("att_max")
        hid_done = sem("hid_done")
        att_psum = sem("att_psum")
        att_step = sem("att_step")
        att_exp = sem("att_exp")
        att_T_psum = sem("att_T_psum")
        att_T_done = sem("att_T_done")
        agg_psum = sem("agg_psum")
        agg_done = sem("agg_done")
        rows_stored = sem("rows_stored")
        block = c.enter_context(nc.Block())

        @block.sync
        def _(sp):
            for dst, src in ((cond_T, a["cond_T"]), (cw_T, a["cw_T"]), (fside, a["fside"].partition_broadcast(P)),
                             (w0, a["w0"]), (w1, a["w1"]), (w2, a["w2"]), (b0, a["b0"]), (b1, a["b1"]),
                             (b2, a["b2"].partition_broadcast(P)), (kern, a["kern"]), (kern_b, a["kern_b"]),
                             (ident, a["ident"])):
                sp.dma_start(dst[:], src).then_inc(params_loaded, 16)
            sp.wait_ge(ctx_added, 1)
            sp.dma_start(ctx_rows, ctx_sb[:]).then_inc(rows_stored, 16)
            sp.wait_ge(agg_done, 3)
            sp.dma_start(aggw_rows, aggw_sb[:]).then_inc(rows_stored, 16)
            sp.dma_start(aggb_rows, aggb_sb[:]).then_inc(rows_stored, 16)
            sp.wait_ge(rows_stored, 48)

        @block.gpsimd
        def _(pool):
            pool.memset(conv_f[:], 0.0).then_inc(conv_zeroed, 1)

        @block.scalar
        def _(act):
            act.wait_ge(conv_zeroed, 1)
            for b in range(TB):
                for g in range(CGROUPS):
                    r = S * b + CG * g
                    act.dma_start(conv_f[r:r + CG, :, r:r + CG],
                                  a["conv_w"][CG * g:CG * (g + 1)]).then_inc(conv_loaded, 16)
            act.wait_ge(conv_loaded, 16 * TB * CGROUPS)
            act.activation(conv_w[:, 0], conv_f[:], ACT.Copy).then_inc(conv_hi, 1)
            for n, bias in enumerate((b0, b1)):
                act.wait_ge(hid_psum, n + 1)
                act.activation(hid[:, n], bank[1 + n][:, 0:B], ACT.Gelu, bias=bias[:, 0:1]).then_inc(hid_done, 1)
            act.wait_ge(att_step, 2)
            act.activation(att[:], att[:], ACT.Exp).then_inc(att_exp, 1)

        @block.tensor
        def _(pe):
            pe.wait_ge(params_loaded, 16 * 12)
            pe.matmul(bank[0][:, 0:S], cond_T[:], cw_T[:], start=True, stop=True).then_inc(ctx_psum, 1)
            pe.matmul(bank[1][:, 0:B], w0[:], cond_T[:], start=True, stop=True).then_inc(hid_psum, 1)
            pe.wait_ge(hid_done, 1)
            pe.matmul(bank[2][:, 0:B], w1[:], hid[:, 0], start=True, stop=True).then_inc(hid_psum, 1)
            pe.wait_ge(hid_done, 2)
            pe.matmul(bank[3][:, 0:COND_K], hid[:, 1], w2[:], start=True, stop=True).then_inc(att_psum, 1)
            pe.wait_ge(att_step, 5)
            pe.transpose(bank[4][0:COND_K, 0:B], att[:], ident[:]).then_inc(att_T_psum, 1)
            pe.wait_ge(att_T_done, 1)
            for n in range(2):
                pe.matmul(bank[5 + n][:, :], att_T[:], kern[:, 512 * n:512 * (n + 1)],
                          start=True, stop=True).then_inc(agg_psum, 1)
            pe.matmul(bank[7][:, 0:S], att_T[:], kern_b[:], start=True, stop=True).then_inc(agg_psum, 1)

        @block.vector
        def _(dve):
            dve.wait_ge(ctx_psum, 1)
            dve.tensor_tensor(ctx_sb[:], bank[0][:, 0:S], fside[:], ALU.add).then_inc(ctx_added, 1)
            dve.wait_ge(conv_hi, 1)
            dve.tensor_tensor(conv_w[:, 1], conv_f[:], conv_w[:, 0], ALU.subtract).then_inc(conv_lo, 1)
            dve.wait_ge(att_psum, 1)
            dve.tensor_tensor(att[:], bank[3][:, 0:COND_K], b2[:], ALU.add).then_inc(att_step, 1)
            dve.wait_ge(att_step, 1)
            dve.tensor_reduce(stat[:, 0:1], att[:], AX.X, ALU.max).then_inc(att_max, 1)
            dve.wait_ge(att_max, 1)
            dve.tensor_scalar(att[:], att[:], stat[:, 0:1], None, ALU.subtract).then_inc(att_step, 1)
            dve.wait_ge(att_exp, 1)
            dve.reduce_sum(stat[:, 1:2], att[:], AX.X).then_inc(att_step, 1)
            dve.wait_ge(att_step, 3)
            dve.reciprocal(stat[:, 2:3], stat[:, 1:2]).then_inc(att_step, 1)
            dve.wait_ge(att_step, 4)
            dve.tensor_scalar(att[:], att[:], stat[:, 2:3], None, ALU.mult).then_inc(att_step, 1)
            dve.wait_ge(att_T_psum, 1)
            dve.tensor_copy(att_T[:], bank[4][0:COND_K, 0:B]).then_inc(att_T_done, 1)
            for n in range(2):
                dve.wait_ge(agg_psum, n + 1)
                dve.tensor_copy(aggw_sb[:, 512 * n:512 * (n + 1)], bank[5 + n][:, :]).then_inc(agg_done, 1)
            dve.wait_ge(agg_psum, 3)
            dve.tensor_copy(aggb_sb[:], bank[7][:, 0:S]).then_inc(agg_done, 1)


def conv_and_dequant(nc, a, bank, x1, hT, conv_w, ctx_rows, w_codes, w_split):
    with ExitStack() as c:
        def sb(name, shape, dt=F32):
            return c.enter_context(nc.sbuf_tensor(name, shape, dt))

        def sem(name):
            return c.enter_context(nc.semaphore(name))

        ctx_bc = sb("ctx_bc", [P, TOKENS])
        x_hl = sb("x_hl", [P, 2, 2, XP], F16)
        h_f = sb("h_f", [P, 2, KT, P])
        codes = sb("codes", [P, 2, QSTEP + WSTEP], I32)
        w_f = sb("w_f", [P, 2, WSTEP])
        wq16 = sb("wq16", [P, 2, QSTEP], F16)
        w_hl = sb("w_hl", [P, 2, 2, WSTEP], F16)

        pads_zeroed = sem("pads_zeroed")
        ctx_loaded = sem("ctx_loaded")
        x_loaded = sem("x_loaded")
        codes_loaded = [sem(f"codes_loaded{n}") for n in range(2)]
        w_stored = [sem(f"w_stored{n}") for n in range(2)]
        x_hi = sem("x_hi")
        x_lo = sem("x_lo")
        conv_psum = sem("conv_psum")
        h_added = sem("h_added")
        h_hi = sem("h_hi")
        h_lo = sem("h_lo")
        w_dequant = sem("w_dequant")
        w_hi = sem("w_hi")
        w_lo = sem("w_lo")
        block = c.enter_context(nc.Block())
        ROUNDS = TILES // 2

        x_rows = a["x"].rearrange("(t p) l -> t p l", p=P)

        def x_cols(n):
            return x_hl[:, n, :, PAD:PAD + D]

        @block.sync
        def _(sp):
            def load_x(r):
                sp.dma_start(x1[:, bass.ds(2 * r, 2)], x_rows[bass.ds(2 * r, 2)].rearrange("t p l -> p t l")).then_inc(x_loaded, 16)

            def load(t, n):
                sp.dma_start(codes[:, n], a["codes"][bass.ds(t, 1)].rearrange("t p n -> p (t n)")).then_inc(codes_loaded[n], 16)
                sp.dma_start(w_f[:, n], a["scales"][bass.ds(t, 1)].rearrange("t n -> (t n)")
                             .partition_broadcast(P)).then_inc(codes_loaded[n], 16)

            def store(t, n):
                sp.wait_ge(w_lo, t + 1)
                sp.dma_start(w_codes[:, bass.ds(t * QSTEP, QSTEP)], wq16[:, n]).then_inc(w_stored[n], 16)
                sp.dma_start(w_split[:, :, bass.ds(t * WSTEP, WSTEP)], w_hl[:, n]).then_inc(w_stored[n], 16)

            load_x(0)
            for n in range(2):
                load(n, n)
            sp.dma_start(ctx_bc[:], ctx_rows.rearrange("b s -> (b s)").partition_broadcast(P)).then_inc(ctx_loaded, 16)
            with sp.Fori(0, ROUNDS - 1) as r:
                sp.wait_ge(x_hi, 2 * r + 1)
                load_x(r + 1)
                for n in range(2):
                    store(2 * r + n, n)
                    load(2 * r + n + 2, n)
            for n in range(2):
                store(TILES - 2 + n, n)
            for n in range(2):
                sp.wait_ge(w_stored[n], 32 * ROUNDS)

        @block.scalar
        def _(act):
            def split_x(t, r, n):
                act.wait_ge(x_loaded, 16 * (r + 1))
                act.activation(x_hl[:, n, 0, PAD:PAD + D], x1[:, bass.ds(t, 1)].rearrange("p t l -> p (t l)"),
                               ACT.Copy).then_inc(x_hi, 1)

            def rest(t, r, n, first):
                act.wait_ge(w_dequant, t + 1)
                act.activation(w_hl[:, n, 0], w_f[:, n], ACT.Copy, scale=WSCALE).then_inc(w_hi, 1)
                act.wait_ge(h_added, t + 1)
                act.activation(hT[:, :, 0, bass.ds(t * P, P)], h_f[:, n], ACT.Copy).then_inc(h_hi, 1)

            act.wait_ge(pads_zeroed, 1)
            split_x(0, 0, 0)
            split_x(1, 0, 1)
            for n in range(2):
                rest(n, 0, n, True)
                split_x(n + 2, 1, n)
            with act.Fori(1, ROUNDS - 1) as r:
                for n in range(2):
                    rest(2 * r + n, r, n, False)
                    split_x(2 * r + n + 2, r + 1, n)
            for n in range(2):
                rest(TILES - 2 + n, ROUNDS - 1, n, False)

        @block.gpsimd
        def _(pool):
            def split_x(t, n):
                pool.wait_ge(x_hi, t + 1)
                pool.tensor_tensor(x_hl[:, n, 1, PAD:PAD + D], x1[:, bass.ds(t, 1)].rearrange("p t l -> p (t l)"),
                                   x_hl[:, n, 0, PAD:PAD + D], ALU.subtract).then_inc(x_lo, 1)

            def split_h(t, n):
                pool.wait_ge(h_hi, t + 1)
                pool.tensor_tensor(hT[:, :, 1, bass.ds(t * P, P)], h_f[:, n], hT[:, :, 0, bass.ds(t * P, P)],
                                   ALU.subtract).then_inc(h_lo, 1)

            pool.memset(x_hl[:], 0.0).then_inc(pads_zeroed, 1)
            for n in range(2):
                split_x(n, n)
            with pool.Fori(0, ROUNDS - 1) as r:
                for n in range(2):
                    split_h(2 * r + n, n)
                    split_x(2 * r + n + 2, n)
            for n in range(2):
                split_h(TILES - 2 + n, n)

        @block.vector
        def _(dve):
            def work(t, r, n, first):
                dve.wait_ge(codes_loaded[n], 32 * (r + 1))
                if not first:
                    dve.wait_ge(w_stored[n], 32 * r)
                dve.scalar_tensor_tensor(out=w_f[:, n], in0=codes[:, n, QSTEP:], scalar=-8.0, in1=w_f[:, n],
                                         op0=ALU.add, op1=ALU.mult).then_inc(w_dequant, 1)
                dve.tensor_scalar(wq16[:, n], codes[:, n, 0:QSTEP], -8.0, None, ALU.add)
                dve.wait_ge(w_hi, t + 1)
                dve.scalar_tensor_tensor(out=w_hl[:, n, 1], in0=w_f[:, n], scalar=WSCALE, in1=w_hl[:, n, 0],
                                         op0=ALU.mult, op1=ALU.subtract).then_inc(w_lo, 1)
                dve.wait_ge(conv_psum, t + 1)
                if not first:
                    dve.wait_ge(h_lo, t - 1)
                dve.tensor_tensor(h_f[:, n], bank[n][:].rearrange("p (k t) -> p k t", k=KT),
                                  ctx_bc[:, bass.ds(t * P, P)].unsqueeze(1).broadcast_to([P, KT, P]),
                                  ALU.add).then_inc(h_added, 1)

            dve.wait_ge(ctx_loaded, 16)
            for n in range(2):
                work(n, 0, n, True)
            with dve.Fori(1, ROUNDS) as r:
                for n in range(2):
                    work(2 * r + n, r, n, False)

        @block.tensor
        def _(pe):
            def conv(t, n, first):
                pe.wait_ge(x_lo, t + 1)
                if not first:
                    pe.wait_ge(h_added, t - 1)
                for k in range(KT):
                    for tap in range(TAPS):
                        for xp, wp in PASSES:
                            mm = pe.matmul(bank[n][:, k * P:(k + 1) * P], x_hl[:, n, xp, k * P + tap:k * P + tap + P],
                                           conv_w[:, wp, tap], start=tap == 0 and (xp, wp) == PASSES[0],
                                           stop=tap == TAPS - 1 and (xp, wp) == PASSES[-1])
                mm.then_inc(conv_psum, 1)

            for n in range(2):
                conv(n, n, True)
            with pe.Fori(1, ROUNDS) as r:
                for n in range(2):
                    conv(2 * r + n, n, False)


def attention(nc, c, a, bank, x1, hT, w_codes, w_split):
    def sb(name, shape, dt=F32):
        return c.enter_context(nc.sbuf_tensor(name, shape, dt))

    def sem(name):
        return c.enter_context(nc.semaphore(name))

    STEPS = NKV * CHUNKS
    w_q = sb("w_q", [P, WQ], F16)
    w_g = sb("w_g", [P, 2, WKVO], F16)
    q_scales = sb("q_scales", [P, NKV, 4, KT])
    q_sum = sb("q_sum", [P, 2, 2, CHUNK])
    q_hl = sb("q_hl", [P, 2, RF, CHUNK], F16)
    k_hl = sb("k_hl", [P, 2, CHUNK], F16)
    v_hl = sb("v_hl", [P, 2, CT, HD], F16)
    o_hl = sb("o_hl", [P, 2, CT, RF, P], F16)
    pad_hl = sb("pad_hl", [P, 2 * CT * RF, TB, S], F16)
    prod = sb("prod", [P, 2, 2, CHUNK])
    y_hl = sb("y_hl", [P, 2, CHUNK], F16)
    k_prod = sb("k_prod", [P, 2, CHUNK])
    sc = sb("sc", [P, CHUNK])
    p_hl = sb("p_hl", [P, 2, CHUNK], F16)
    pT_hl = sb("pT_hl", [P, 2 * CT * RF, S], F16)
    stats = sb("stats", [P, 3, CT * RF])
    cos2 = sb("cos2", [P, S])
    sin2 = sb("sin2", [P, S])
    cos_k = sb("cos_k", [P, S])
    sin_k = sb("sin_k", [P, S])
    mask_f = sb("mask_f", [P, S])
    ident_f = sb("ident_f", [P, P])
    mask_b = sb("mask_b", [P, CT * RF, S], BF16)
    ident_b = sb("ident_b", [P, P], BF16)

    consts_loaded = sem("consts_loaded")
    consts_ready = sem("consts_ready")
    pad_zeroed = sem("pad_zeroed")
    wk_loaded = sem("wk_loaded")
    wq_loaded = sem("wq_loaded")
    wv_loaded = sem("wv_loaded")
    wo_loaded = sem("wo_loaded")
    k_psum = sem("k_psum")
    q_psum = sem("q_psum")
    q_scaled = sem("q_scaled")
    q_summed = sem("q_summed")
    q_total = sem("q_total")
    q_last_total = sem("q_last_total")
    v_psum = sem("v_psum")
    scores_psum = sem("scores_psum")
    pv_psum = sem("pv_psum")
    o_psum = sem("o_psum")
    k_products = sem("k_products")
    k_rotated = sem("k_rotated")
    k_hi = sem("k_hi")
    k_ready = sem("k_ready")
    q_products = sem("q_products")
    q_rotated = sem("q_rotated")
    q_hi = sem("q_hi")
    q_lo = sem("q_lo")
    q_last_lo = sem("q_last_lo")
    q_moved = sem("q_moved")
    q_ready = sem("q_ready")
    v_hi = sem("v_hi")
    v_ready = sem("v_ready")
    sc_read = sem("sc_read")
    max_done = sem("max_done")
    shifted = sem("shifted")
    exp_done = sem("exp_done")
    sum_done = sem("sum_done")
    inv_done = sem("inv_done")
    probs = sem("probs")
    probs_hi = sem("probs_hi")
    probs_lo = sem("probs_lo")
    probs_T = sem("probs_T")
    probs_padded = sem("probs_padded")
    out_hi = sem("out_hi")
    out_ready = sem("out_ready")
    x1_added = sem("x1_added")
    block = c.enter_context(nc.Block())

    def w_cols(part, col, n):
        return w_g[:, part, col:col + n]

    def head_of(n):
        return n // CHUNKS if isinstance(n, int) else n >> 3

    def q_scale(n, tile, kt):
        head = head_of(n) if isinstance(n, int) else head_of(n) & (NKV - 1)
        return q_scales[:, bass.ds(head, 1), tile, kt]

    def table(t, parts=slice(0, P)):
        n = parts.stop - parts.start
        return t[parts, :].unsqueeze(1).broadcast_to([n, CHUNK // S, S])

    def by_s(ap):
        return ap.rearrange("p (b s) -> p b s", s=S)

    @block.sync
    def _(sp):
        for dst, src in ((cos2, a["cos2"]), (sin2, a["sin2"]), (cos_k, a["cos_k"]), (sin_k, a["sin_k"]),
                         (q_scales, a["q_scales"]), (mask_f, a["mask"]), (ident_f, a["ident"])):
            sp.dma_start(dst[:], src).then_inc(consts_loaded, 16)

        def load(cols, src, at, loaded):
            sp.dma_start(cols, src[..., bass.ds(at, cols.shape[-1])]).then_inc(loaded, 16)

        def load_k(g):
            load(w_g[:, :, WK:WV], w_split, g * WKVO + WK, wk_loaded)

        def load_q(g):
            load(w_q[:], w_codes, g * WQ, wq_loaded)

        def load_v(g):
            load(w_g[:, :, WV:WO], w_split, g * WKVO + WV, wv_loaded)

        def load_o(g):
            load(w_g[:, :, WO:WKVO], w_split, g * WKVO + WO, wo_loaded)

        load_k(0)
        load_q(0)
        load_v(0)
        load_o(0)
        with sp.Fori(1, NKV) as g:
            sp.wait_ge(q_psum, 4 * KT * CHUNKS * g)
            load_q(g)
            sp.wait_ge(k_psum, CHUNKS * g)
            load_k(g)
            sp.wait_ge(v_psum, CHUNKS * g)
            load_v(g)
            sp.wait_ge(o_psum, CT * CHUNKS * g)
            load_o(g)

    @block.tensor
    def _(pe):
        def tok(n):
            return n % CHUNKS * CHUNK if isinstance(n, int) else (n & (CHUNKS - 1)) * CHUNK

        def project_k(n):
            t0 = tok(n)
            pe.wait_ge(wk_loaded, 16 * (head_of(n) + 1))
            i = 0
            for kt in range(KT):
                for wp, hp in PASSES:
                    mm = pe.matmul(bank[4][:], w_cols(wp, WK + kt * HD, HD), hT[:, kt, hp, bass.ds(t0, CHUNK)],
                                   start=i == 0, stop=i == 3 * KT - 1)
                    i += 1
            mm.then_inc(k_psum, 1)

        def project_q(n, pair):
            t0 = tok(n)
            if pair == 0:
                pe.wait_ge(wq_loaded, 16 * (head_of(n) + 1))
            for tile in (2 * pair, 2 * pair + 1):
                for kt in range(KT):
                    if tile:
                        pe.wait_ge(q_scaled if kt < 2 else q_summed, 8 * n + 2 * tile - 1 + kt % 2)
                    for hp in range(2):
                        mm = pe.matmul(bank[kt][:], w_q[:, kt * 512 + tile * P:kt * 512 + (tile + 1) * P],
                                       hT[:, kt, hp, bass.ds(t0, CHUNK)], start=hp == 0, stop=hp == 1)
                    mm.then_inc(q_psum, 1)

        def project_v(n):
            t0 = tok(n)
            pe.wait_ge(wv_loaded, 16 * (head_of(n) + 1))
            for j in range(CT):
                i = 0
                for kt in range(KT):
                    for hp, wp in PASSES:
                        mm = pe.matmul(bank[5][:, j * HD:(j + 1) * HD], hT[:, kt, hp, bass.ds(t0 + j * P, P)],
                                       w_cols(wp, WV + kt * HD, HD), start=i == 0, stop=i == 3 * KT - 1)
                        i += 1
                        if j < CT - 1 or i < 3 * KT:
                            yield
            mm.then_inc(v_psum, 1)
            yield

        def scores(i):
            pe.wait_ge(k_ready, i + 1)
            pe.wait_ge(q_ready, 2 * i + 2)
            pe.matmul(bank[6][:], ident_b[:], mask_b[:].rearrange("p n s -> p (n s)"), start=True, stop=False,
                      skip_group_check=True)
            for j in range(CT):
                for kp, qp in PASSES:
                    for b in range(TB):
                        t = j * P + b * S
                        mm = pe.matmul(bank[6][b * S:(b + 1) * S, j * P:(j + 1) * P], k_hl[:, kp, t:t + S],
                                       q_hl[:, qp, :, t:t + S], start=False, stop=(kp, qp) == PASSES[-1] and j == CT - 1,
                                       skip_group_check=True)
            mm.then_inc(scores_psum, 1)

        def values(i, n=None, v=None):
            pe.wait_ge(probs_padded, i + 1)
            pe.wait_ge(v_ready, i + 1)
            if n is not None:
                pe.wait_ge(q_scaled, 8 * n + 8)
                pe.wait_ge(q_summed, 8 * n + 8)
            for j in range(CT):
                for m, (vp, pp) in enumerate(PASSES):
                    mm = pe.matmul(bank[j][:], v_hl[:, vp, j],
                                   pad_hl[:, (pp * CT + j) * RF:(pp * CT + j + 1) * RF].rearrange("p n b s -> p (n b s)"),
                                   start=m == 0, stop=m == 2)
                    if m == 2:
                        mm.then_inc(pv_psum, 1)
                    if v is not None:
                        for _ in range(KT):
                            next(v)

        def output(i, tiles, busy=True):
            if tiles[0] == 0:
                pe.wait_ge(wo_loaded, 16 * (head_of(i) + 1))
            for j in tiles:
                pe.wait_ge(out_ready, CT * i + j + 1)
                if j == 0 and busy:
                    pe.wait_ge(v_ready, i + 2)
                if j >= 2:
                    pe.wait_ge(x1_added, CT * i + j - 1)
                n = 0
                for h in range(RF):
                    for op, wp in PASSES:
                        mm = pe.matmul(bank[5 + j % 2 * 2][:], o_hl[:, op, j, h], w_o(wp, h), start=n == 0, stop=n == 3 * RF - 1)
                        n += 1
                mm.then_inc(o_psum, 1)

        def w_o(part, h):
            return w_cols(part, WO + h * D, D)

        pe.wait_ge(consts_ready, 2)
        project_k(0)
        project_q(0, 0)
        project_q(0, 1)
        for _ in project_v(0):
            pass
        scores(0)
        project_k(1)
        project_q(1, 0)
        project_q(1, 1)
        values(0, 1, project_v(1))
        with pe.Fori(1, STEPS - 1) as i:
            scores(i)
            project_k(i + 1)
            pe.wait_ge(out_ready, CT * i)
            project_q(i + 1, 0)
            output(i - 1, (0, 1))
            project_q(i + 1, 1)
            output(i - 1, (2, 3))
            pe.wait_ge(x1_added, CT * i - 1)
            values(i, i + 1, project_v(i + 1))
            pe.wait_ge(x1_added, CT * i)
        scores(STEPS - 1)
        output(STEPS - 2, range(CT))
        values(STEPS - 1)
        pe.wait_ge(x1_added, CT * (STEPS - 1))
        output(STEPS - 1, range(CT), busy=False)

    @block.vector
    def _(dve):
        def rotate_k(n):
            dve.wait_ge(k_psum, n + 1)
            dve.tensor_tensor(by_s(k_prod[:, 0]), by_s(bank[4][:]), table(cos_k), ALU.mult)
            for h in range(2):
                src = slice(64 * (1 - h), 64 * (2 - h))
                ins = dve.tensor_tensor(by_s(k_prod[64 * h:64 * (h + 1), 1]), by_s(bank[4][src, :]), table(sin_k, src), ALU.mult)
            ins.then_inc(k_products, 1)

        def sum_q(n, tile):
            for kt in range(2, KT):
                half = q_sum[:, tile % 2, kt - 2]
                dve.wait_ge(q_psum, 4 * KT * n + KT * tile + kt + 1)
                dve.wait_ge(q_scaled, 8 * n + 2 * tile + kt - 1)
                dve.scalar_tensor_tensor(out=half, in0=bank[kt][:], scalar=q_scale(n, tile, kt), in1=half,
                                         op0=ALU.mult, op1=ALU.add).then_inc(q_summed, 1)

        def total_last(n):
            dve.wait_ge(q_summed, 8 * n + 8)
            dve.tensor_tensor(q_sum[:, 1, 0], q_sum[:, 1, 0], q_sum[:, 1, 1], ALU.add).then_inc(q_last_total, 1)

        def rotate_q(n, stage):
            eo = stage % 2
            if stage == 0:
                dve.wait_ge(q_total, 3 * n + 2)
            if stage == 2:
                dve.wait_ge(q_total, 3 * n + 3)
                dve.wait_ge(q_last_total, n + 1)
            if stage >= 2:
                dve.wait_ge(q_lo, 3 * n + stage - 1)
            dve.tensor_tensor(by_s(prod[:, eo, 0]), by_s(q_sum[:, eo, 0]), table(cos2), ALU.mult)
            dve.tensor_tensor(by_s(prod[:, eo, 1]), by_s(q_sum[:, 1 - eo, 0]), table(sin2), ALU.mult).then_inc(q_products, 1)

        def q_low_last(n):
            dve.wait_ge(q_hi, 4 * n + 4)
            dve.tensor_tensor(y_hl[:, 1], prod[:, 1, 0], y_hl[:, 0], ALU.subtract).then_inc(q_last_lo, 1)

        def gather_q(n, pair):
            even, odd = 2 * pair, 2 * pair + 1
            if pair == 0:
                dve.wait_ge(q_lo, 3 * n + 2)
            else:
                dve.wait_ge(q_lo, 3 * n + 3)
                dve.wait_ge(q_last_lo, n + 1)
            dve.tensor_copy(q_hl[0:64, :, odd], q_hl[64:128, :, even]).then_inc(q_moved, 1)
            dve.tensor_copy(q_hl[64:128, :, odd], y_hl[64:128])
            dve.wait_ge(q_moved, 2 * n + pair + 1)
            dve.tensor_copy(q_hl[64:128, :, even], y_hl[0:64]).then_inc(q_ready, 1)

        def finish_v(n):
            dve.wait_ge(v_hi, n + 1)
            dve.scalar_tensor_tensor(out=v_hl[:, 1].rearrange("p j d -> p (j d)"), in0=bank[5][:], scalar=1 / WSCALE,
                                     in1=v_hl[:, 0].rearrange("p j d -> p (j d)"), op0=ALU.mult,
                                     op1=ALU.subtract).then_inc(v_ready, 1)

        def softmax_exp(i):
            dve.wait_ge(scores_psum, i + 1)
            dve.transpose(sc[:], bank[6][:]).then_inc(sc_read, 1)
            dve.wait_ge(sc_read, i + 1)
            dve.tensor_reduce(stats[:, 0], by_s(sc[:]), AX.X, ALU.max).then_inc(max_done, 1)
            dve.wait_ge(max_done, i + 1)
            dve.tensor_tensor(by_s(sc[:]), by_s(sc[:]), stats[:, 0].unsqueeze(2).broadcast_to([P, CT * RF, S]),
                              ALU.subtract).then_inc(shifted, 1)

        def softmax_norm(i):
            dve.wait_ge(exp_done, i + 1)
            dve.reduce_sum(stats[:, 1], by_s(sc[:]), AX.X).then_inc(sum_done, 1)
            dve.wait_ge(sum_done, i + 1)
            dve.reciprocal(stats[:, 2], stats[:, 1]).then_inc(inv_done, 1)
            dve.wait_ge(inv_done, i + 1)
            dve.tensor_tensor(by_s(sc[:]), by_s(sc[:]), stats[:, 2].unsqueeze(2).broadcast_to([P, CT * RF, S]),
                              ALU.mult).then_inc(probs, 1)

        def softmax_T(i):
            dve.wait_ge(probs_lo, i + 1)
            dve.transpose(pT_hl[:].rearrange("p n s -> p (n s)"), p_hl[:].rearrange("p h n -> p (h n)")).then_inc(probs_T, 1)

        def finish_out(i, tiles):
            for j in tiles:
                dve.wait_ge(out_hi, CT * i + j + 1)
                dve.tensor_tensor(o_hl[:, 1, j].rearrange("p h t -> p (h t)"), bank[j][:],
                                  o_hl[:, 0, j].rearrange("p h t -> p (h t)"), ALU.subtract).then_inc(out_ready, 1)

        def add_out(i, j):
            tile = (i % CHUNKS if isinstance(i, int) else i & (CHUNKS - 1)) * CT + j
            dst = x1[:, bass.ds(tile, 1)].rearrange("p t l -> p (t l)")
            dve.wait_ge(o_psum, CT * i + j + 1)
            dve.scalar_tensor_tensor(out=dst, in0=bank[5 + j % 2 * 2][:], scalar=1 / WSCALE, in1=dst,
                                     op0=ALU.mult, op1=ALU.add).then_inc(x1_added, 1)

        dve.wait_ge(consts_loaded, 16 * 7)
        dve.tensor_copy(mask_b[:], mask_f[:].unsqueeze(1).broadcast_to([P, CT * RF, S])).then_inc(consts_ready, 1)
        dve.tensor_copy(ident_b[:], ident_f[:]).then_inc(consts_ready, 1)
        def body(i, n, prior):
            def add(j):
                if prior is not None:
                    add_out(prior, j)

            softmax_exp(i)
            rotate_k(n)
            sum_q(n, 0)
            sum_q(n, 1)
            softmax_norm(i)
            rotate_q(n, 0)
            add(0)
            rotate_q(n, 1)
            softmax_T(i)
            sum_q(n, 2)
            add(1)
            sum_q(n, 3)
            gather_q(n, 0)
            total_last(n)
            add(2)
            rotate_q(n, 2)
            rotate_q(n, 3)
            add(3)
            finish_out(i, (0,))
            q_low_last(n)
            gather_q(n, 1)
            finish_out(i, (1, 2, 3))
            finish_v(n)

        rotate_k(0)
        sum_q(0, 0)
        sum_q(0, 1)
        rotate_q(0, 0)
        rotate_q(0, 1)
        sum_q(0, 2)
        sum_q(0, 3)
        total_last(0)
        gather_q(0, 0)
        rotate_q(0, 2)
        rotate_q(0, 3)
        q_low_last(0)
        gather_q(0, 1)
        finish_v(0)
        body(0, 1, None)
        with dve.Fori(1, STEPS - 1) as i:
            body(i, i + 1, i - 1)
        softmax_exp(STEPS - 1)
        softmax_norm(STEPS - 1)
        softmax_T(STEPS - 1)
        for j in range(CT):
            add_out(STEPS - 2, j)
        finish_out(STEPS - 1, range(CT))
        for j in range(CT):
            add_out(STEPS - 1, j)

    @block.gpsimd
    def _(pool):
        def rotate_k(n):
            pool.wait_ge(k_products, n + 1)
            pool.tensor_tensor(k_prod[:, 0], k_prod[:, 0], k_prod[:, 1], ALU.add).then_inc(k_rotated, 1)

        def finish_k(n):
            pool.wait_ge(k_hi, n + 1)
            pool.tensor_tensor(k_hl[:, 1], k_prod[:, 0], k_hl[:, 0], ALU.subtract).then_inc(k_ready, 1)

        def total_q(n, tile):
            pool.wait_ge(q_summed, 8 * n + 2 * tile + 2)
            pool.tensor_tensor(q_sum[:, tile % 2, 0], q_sum[:, tile % 2, 0], q_sum[:, tile % 2, 1],
                               ALU.add).then_inc(q_total, 1)

        def rotate_q(n, pair):
            for eo in range(2):
                pool.wait_ge(q_products, 4 * n + 2 * pair + eo + 1)
                pool.tensor_tensor(prod[:, eo, 0], prod[:, eo, 0], prod[:, eo, 1],
                                   ALU.add if eo else ALU.subtract).then_inc(q_rotated, 1)
            for eo in range(2 - pair):
                dst = y_hl if eo else q_hl[:, :, 2 * pair]
                pool.wait_ge(q_hi, 4 * n + 2 * pair + eo + 1)
                pool.tensor_tensor(dst[:, 1], prod[:, eo, 0], dst[:, 0], ALU.subtract).then_inc(q_lo, 1)

        def probs_low(i):
            pool.wait_ge(probs_hi, i + 1)
            pool.tensor_tensor(p_hl[:, 1], sc[:], p_hl[:, 0], ALU.subtract).then_inc(probs_lo, 1)

        pool.memset(pad_hl[:], 0.0).then_inc(pad_zeroed, 1)
        rotate_k(0)
        total_q(0, 0)
        total_q(0, 1)
        finish_k(0)
        rotate_q(0, 0)
        total_q(0, 2)
        rotate_q(0, 1)
        with pool.Fori(0, STEPS - 1) as i:
            rotate_k(i + 1)
            total_q(i + 1, 0)
            finish_k(i + 1)
            total_q(i + 1, 1)
            probs_low(i)
            rotate_q(i + 1, 0)
            total_q(i + 1, 2)
            rotate_q(i + 1, 1)
        probs_low(STEPS - 1)

    @block.scalar
    def _(act):
        def exp(i):
            act.wait_ge(shifted, i + 1)
            act.activation(sc[:], sc[:], ACT.Exp, scale=SM_SCALE).then_inc(exp_done, 1)

        def k_high(n):
            act.wait_ge(k_rotated, n + 1)
            act.activation(k_hl[:, 0], k_prod[:, 0], ACT.Copy).then_inc(k_hi, 1)

        def probs_high(i):
            act.wait_ge(probs, i + 1)
            act.activation(p_hl[:, 0], sc[:], ACT.Copy).then_inc(probs_hi, 1)

        def scale_q(n, tile):
            if tile >= 2:
                act.wait_ge(q_products, 4 * n + 2)
            for kt in range(2):
                act.wait_ge(q_psum, 4 * KT * n + KT * tile + kt + 1)
                act.activation(q_sum[:, tile % 2, kt], bank[kt][:], ACT.Copy, scale=q_scale(n, tile, kt)).then_inc(q_scaled, 1)

        def q_high(n, stage):
            act.wait_ge(q_rotated, 4 * n + stage + 1)
            if stage == 3:
                act.wait_ge(q_ready, 2 * n + 1)
            dst = y_hl if stage % 2 else q_hl[:, :, stage]
            act.activation(dst[:, 0], prod[:, stage % 2, 0], ACT.Copy).then_inc(q_hi, 1)

        def pad(i):
            act.wait_ge(probs_T, i + 1)
            for b in range(TB):
                ins = act.activation(pad_hl[b * S:(b + 1) * S, :, b], pT_hl[b * S:(b + 1) * S], ACT.Copy)
            ins.then_inc(probs_padded, 1)

        def v_high(n):
            act.wait_ge(v_psum, n + 1)
            act.activation(v_hl[:, 0].rearrange("p j d -> p (j d)"), bank[5][:], ACT.Copy, scale=1 / WSCALE).then_inc(v_hi, 1)

        def out_high(i, j):
            act.wait_ge(pv_psum, CT * i + j + 1)
            act.activation(o_hl[:, 0, j].rearrange("p h t -> p (h t)"), bank[j][:], ACT.Copy).then_inc(out_hi, 1)

        def body(i, n):
            exp(i)
            scale_q(n, 0)
            scale_q(n, 1)
            k_high(n)
            probs_high(i)
            q_high(n, 0)
            scale_q(n, 2)
            scale_q(n, 3)
            q_high(n, 1)
            pad(i)
            out_high(i, 0)
            q_high(n, 2)
            q_high(n, 3)
            out_high(i, 1)
            out_high(i, 2)
            out_high(i, 3)
            v_high(n)

        act.wait_ge(consts_loaded, 16 * 7)
        act.wait_ge(pad_zeroed, 1)
        scale_q(0, 0)
        scale_q(0, 1)
        k_high(0)
        q_high(0, 0)
        scale_q(0, 2)
        scale_q(0, 3)
        q_high(0, 1)
        q_high(0, 2)
        q_high(0, 3)
        v_high(0)
        body(0, 1)
        with act.Fori(1, STEPS - 1) as i:
            body(i, i + 1)
        exp(STEPS - 1)
        probs_high(STEPS - 1)
        pad(STEPS - 1)
        for j in range(CT):
            out_high(STEPS - 1, j)


def mix_and_ffn(nc, c, a, bank, x1, aggb_rows, aggw_rows, out):
    def sb(name, shape, dt=F32):
        return c.enter_context(nc.sbuf_tensor(name, shape, dt))

    def sem(name):
        return c.enter_context(nc.semaphore(name))

    mixw_f = sb("mixw_f", [P, TILES, P])
    mixw = sb("mixw", [P, 2, TILES, P], F16)
    aggb = sb("aggb", [P, TOKENS])
    base_f = sb("base_f", [P, KT, D])
    base = sb("base", [P, 2, KT, D], F16)
    gl_f = sb("gl_f", [P, KT, GL])
    gl = sb("gl", [P, 2, KT, GL], F16)
    lb_f = sb("lb_f", [EH, 2, D])
    lb = sb("lb", [EH, 2, 2, D], F16)
    ident = sb("ident_m", [P, P])
    iota = sb("iota", [P, EXPERTS])
    x_hl = sb("xm_hl", [P, 2, 2, D], F16)
    y_f = sb("y_f", [P, 2, D])
    y_hl = sb("ym_hl", [P, 2, 2, D], F16)
    logits = sb("logits", [P, 2, EXPERTS])
    top = sb("top", [P, 2, 8])
    top_at = sb("top_at", [P, 2, 8], U32)
    topv = sb("topv", [P, 2, 8])
    gates = sb("gates", [P, 2, 2, EXPERTS])
    lora = sb("lora", [P, 2, ER])
    loraT = sb("loraT", [EH, 2, 2, 2, P], F16)
    res = sb("res", [P, 2, D])

    mixw_zeroed = sem("mixw_zeroed")
    mixw_loaded = sem("mixw_loaded")
    w_loaded = sem("w_loaded")
    w_his = sem("w_his")
    w_ready = sem("w_ready")
    xs_hi = sem("xs_hi")
    xs_ready = sem("xs_ready")
    y_psum = sem("y_psum")
    y_added = sem("y_added")
    y_hi = sem("y_hi")
    y_ready = sem("y_ready")
    gl_psum = sem("gl_psum")
    base_psum = sem("base_psum")
    gate_step = sem("gate_step")
    gate_exp = sem("gate_exp")
    lora_gated = sem("lora_gated")
    loraT_psum = sem("loraT_psum")
    loraT_hi = sem("loraT_hi")
    loraT_ready = sem("loraT_ready")
    ffn_psum = sem("ffn_psum")
    res_done = sem("res_done")
    out_stored = [sem(f"out_stored{n}") for n in range(2)]
    block = c.enter_context(nc.Block())
    ROUNDS = TILES // 2
    GATE_STEPS = 9
    out_rows = out.rearrange("(t p) l -> t p l", p=P)

    def tile_of(t):
        return x1[:, bass.ds(t, 1)].rearrange("p t l -> p (t l)")

    splits = ((base, base_f, FSCALE), (gl, gl_f, FSCALE), (lb, lb_f, FSCALE), (mixw, mixw_f, FSCALE))

    @block.sync
    def _(sp):
        for dst, src in ((base_f, a["base_T"]), (gl_f, a["gl_T"]), (lb_f, a["lb_T"]), (ident, a["ident"]),
                         (iota, a["iota"].partition_broadcast(P))):
            sp.dma_start(dst[:], src).then_inc(w_loaded, 16)
        sp.dma_start(aggb[:], aggb_rows.rearrange("b s -> (b s)").partition_broadcast(P)).then_inc(w_loaded, 16)
        sp.wait_ge(mixw_zeroed, 1)
        for b in range(TB):
            sp.dma_start(mixw_f[b * S:(b + 1) * S, :, b * S:(b + 1) * S],
                         aggw_rows.rearrange("(t b) (i o) -> b i t o", b=TB, i=S)[b]).then_inc(mixw_loaded, 16)
        with sp.Fori(0, ROUNDS) as r:
            for n in range(2):
                t = 2 * r + n
                sp.wait_ge(res_done, t + 1)
                sp.dma_start(out_rows[bass.ds(t, 1)].rearrange("t p l -> p (t l)"), res[:, n]).then_inc(out_stored[n], 16)
        for n in range(2):
            sp.wait_ge(out_stored[n], 16 * ROUNDS)

    @block.tensor
    def _(pe):
        def mix(t, n):
            pe.wait_ge(xs_ready, t + 1)
            for k in range(KT):
                for i, (xp, wp) in enumerate(PASSES):
                    mm = pe.matmul(bank[n][:, k * P:(k + 1) * P], x_hl[:, n, xp, k * P:(k + 1) * P],
                                   mixw[:, wp, bass.ds(t, 1)].rearrange("p t o -> p (t o)"), start=i == 0, stop=i == 2)
            mm.then_inc(y_psum, 1)

        def gate_lora(t, n):
            pe.wait_ge(y_ready, t + 1)
            i = 0
            for k in range(KT):
                for yp, wp in PASSES:
                    mm = pe.matmul(bank[4 + n][:, 0:GL], y_hl[:, n, yp, k * P:(k + 1) * P], gl[:, wp, k],
                                   start=i == 0, stop=i == 3 * KT - 1)
                    i += 1
            mm.then_inc(gl_psum, 1)

        def base_out(t, n, first):
            if not first:
                pe.wait_ge(res_done, t - 1)
            i = 0
            for k in range(KT):
                for yp, wp in PASSES:
                    pe.matmul(bank[2 + n][:], y_hl[:, n, yp, k * P:(k + 1) * P], base[:, wp, k],
                              start=i == 0, stop=False, skip_group_check=True)
                    i += 1

        def lora_transpose(t, n):
            pe.wait_ge(lora_gated, t + 1)
            for h in range(2):
                mm = pe.transpose(bank[6 + n][0:EH, h * P:(h + 1) * P], lora[:, n, h * EH:(h + 1) * EH], ident[:])
            mm.then_inc(loraT_psum, 1)

        def lora_out(t, n):
            pe.wait_ge(loraT_ready, t + 1)
            for h in range(2):
                for i, (lp, wp) in enumerate(PASSES):
                    mm = pe.matmul(bank[2 + n][:], loraT[:, n, lp, h], lb[:, wp, h], start=False,
                                   stop=h == 1 and i == 2, skip_group_check=True)
            mm.then_inc(ffn_psum, 1)

        def body(t, n, first, last):
            gate_lora(t, n)
            if not last:
                mix(t + 1, 1 - n)
            if not (first and n == 0):
                lora_out(t - 1, 1 - n)
            base_out(t, n, first)
            lora_transpose(t, n)

        pe.wait_ge(w_ready, len(splits))
        mix(0, 0)
        for n in range(2):
            body(n, n, True, False)
        with pe.Fori(1, ROUNDS - 1) as r:
            for n in range(2):
                body(2 * r + n, n, False, False)
        for n in range(2):
            body(TILES - 2 + n, n, False, n == 1)
        lora_out(TILES - 1, 1)

    @block.scalar
    def _(act):
        def x_high(t, n):
            act.activation(x_hl[:, n, 0], tile_of(t), ACT.Copy).then_inc(xs_hi, 1)

        def y_high(t, n):
            act.wait_ge(y_added, t + 1)
            act.activation(y_hl[:, n, 0], y_f[:, n], ACT.Copy).then_inc(y_hi, 1)

        def exp(t, n):
            act.wait_ge(gate_step, GATE_STEPS * t + 3)
            act.activation(topv[:, n, 3:4], topv[:, n, 2:3], ACT.Exp).then_inc(gate_exp, 1)

        def lora_high(t, n):
            act.wait_ge(loraT_psum, t + 1)
            act.activation(loraT[:, n, 0], bank[6 + n][0:EH, 0:2 * P].rearrange("p (h t) -> p h t", h=2),
                           ACT.Copy).then_inc(loraT_hi, 1)

        act.wait_ge(w_loaded, 16 * 6)
        for dst, src, scale in splits:
            if src is mixw_f:
                act.wait_ge(mixw_loaded, 16 * TB)
            act.activation(dst[:, 0], src[:], ACT.Copy, scale=scale).then_inc(w_his, 1)
        x_high(0, 0)
        x_high(1, 1)
        y_high(0, 0)
        with act.Fori(0, ROUNDS - 1) as r:
            for n in range(2):
                x_high(2 * r + n + 2, n)
                exp(2 * r + n, n)
                y_high(2 * r + n + 1, 1 - n)
                lora_high(2 * r + n, n)
        exp(TILES - 2, 0)
        y_high(TILES - 1, 1)
        lora_high(TILES - 2, 0)
        exp(TILES - 1, 1)
        lora_high(TILES - 1, 1)

    @block.gpsimd
    def _(pool):
        def x_low(t, n):
            pool.wait_ge(xs_hi, t + 1)
            pool.tensor_tensor(x_hl[:, n, 1], tile_of(t), x_hl[:, n, 0], ALU.subtract).then_inc(xs_ready, 1)

        def y_low(t, n):
            pool.wait_ge(y_hi, t + 1)
            pool.tensor_tensor(y_hl[:, n, 1], y_f[:, n], y_hl[:, n, 0], ALU.subtract).then_inc(y_ready, 1)

        pool.memset(mixw_f[:], 0.0).then_inc(mixw_zeroed, 1)
        x_low(0, 0)
        x_low(1, 1)
        y_low(0, 0)
        with pool.Fori(0, ROUNDS - 1) as r:
            for n in range(2):
                x_low(2 * r + n + 2, n)
                y_low(2 * r + n + 1, 1 - n)
        y_low(TILES - 1, 1)

    @block.vector
    def _(dve):
        def add_bias(t, n):
            dve.wait_ge(y_psum, t + 1)
            dve.scalar_tensor_tensor(out=y_f[:, n].rearrange("p (k t) -> p k t", k=KT),
                                     in0=bank[n][:].rearrange("p (k t) -> p k t", k=KT), scalar=1 / FSCALE,
                                     in1=aggb[:, bass.ds(t * P, P)].unsqueeze(1).broadcast_to([P, KT, P]),
                                     op0=ALU.mult, op1=ALU.add).then_inc(y_added, 1)

        def gate(t, n, last):
            count = [0]

            def step(ins):
                count[0] += 1
                ins.then_inc(gate_step, 1)
                dve.wait_ge(gate_step, GATE_STEPS * t + count[0])

            v = topv[:, n]
            dve.wait_ge(gl_psum, t + 1)
            step(dve.tensor_scalar(logits[:, n], bank[4 + n][:, 0:EXPERTS], 1 / FSCALE, None, ALU.mult))
            dve.memset(v[:, 7:8], 0.0)
            step(dve.max(top[:, n], logits[:, n]))
            step(dve.tensor_tensor(v[:, 2:3], top[:, n, 1:2], top[:, n, 0:1], ALU.subtract))
            dve.memset(v[:, 7:8], 0.0)
            step(dve.max_index(top_at[:, n], top[:, n], logits[:, n]))
            dve.tensor_copy(v[:, 0:2], top_at[:, n, 0:2])
            if not last:
                add_bias(t + 1, 1 - n)
            dve.wait_ge(gate_exp, t + 1)
            step(dve.tensor_scalar(v[:, 4:5], v[:, 3:4], 1.0, None, ALU.add))
            step(dve.reciprocal(v[:, 5:6], v[:, 4:5]))
            step(dve.tensor_tensor(v[:, 6:7], v[:, 3:4], v[:, 5:6], ALU.mult))
            dve.tensor_scalar(gates[:, n, 0], iota[:], v[:, 0:1], v[:, 5:6], ALU.is_equal, ALU.mult)
            step(dve.tensor_scalar(gates[:, n, 1], iota[:], v[:, 1:2], v[:, 6:7], ALU.is_equal, ALU.mult))
            step(dve.tensor_tensor(gates[:, n, 0], gates[:, n, 0], gates[:, n, 1], ALU.add))
            assert count[0] == GATE_STEPS
            dve.scalar_tensor_tensor(out=lora[:, n].rearrange("p (e r) -> p e r", r=RANK),
                                     in0=bank[4 + n][:, EXPERTS:GL].rearrange("p (e r) -> p e r", r=RANK),
                                     scalar=LORA / FSCALE, in1=gates[:, n, 0].unsqueeze(2).broadcast_to([P, EXPERTS, RANK]),
                                     op0=ALU.mult, op1=ALU.mult).then_inc(lora_gated, 1)

        def lora_low(t, n):
            dve.wait_ge(loraT_hi, t + 1)
            dve.tensor_tensor(loraT[:, n, 1], bank[6 + n][0:EH, 0:2 * P].rearrange("p (h t) -> p h t", h=2),
                              loraT[:, n, 0], ALU.subtract).then_inc(loraT_ready, 1)

        def finish(t, r, n, first):
            dve.wait_ge(ffn_psum, t + 1)
            if not first:
                dve.wait_ge(out_stored[n], 16 * r)
            dve.scalar_tensor_tensor(out=res[:, n], in0=bank[2 + n][:], scalar=1 / FSCALE, in1=tile_of(t),
                                     op0=ALU.mult, op1=ALU.add).then_inc(res_done, 1)

        def body(t, r, n, first, second, last):
            gate(t, n, last)
            if n == 1:
                finish(t - 1, r, 0, first)
            elif not first:
                finish(t - 1, r - 1, 1, second)
            lora_low(t, n)

        for k, (dst, src, scale) in enumerate(splits):
            dve.wait_ge(w_his, k + 1)
            dve.scalar_tensor_tensor(out=dst[:, 1], in0=src[:], scalar=scale, in1=dst[:, 0], op0=ALU.mult,
                                     op1=ALU.subtract).then_inc(w_ready, 1)
        add_bias(0, 0)
        for n in range(2):
            body(n, 0, n, True, False, False)
        for n in range(2):
            body(2 + n, 1, n, False, True, False)
        with dve.Fori(2, ROUNDS - 1) as r:
            for n in range(2):
                body(2 * r + n, r, n, False, False, False)
        for n in range(2):
            body(TILES - 2 + n, ROUNDS - 1, n, False, False, n == 1)
        finish(TILES - 1, ROUNDS - 1, 1, False)


def kernel(**inputs):
    import numpy as np
    import concourse.bacc as bacc
    from concourse.bass_utils import run_bass_kernel_spmd

    i = {k: np.asarray(v) for k, v in inputs.items()}

    def cols(codes, perm=None):
        n = codes.shape[1] // NKV
        return codes.reshape(KT, P, NKV, n).transpose(2, 1, 0, 3).reshape(NKV, P, KT * n)

    def split_dims(m, heads):
        rows = m.shape[0]
        if heads == NKV:
            return m.reshape(rows, NKV, HD // 2, 2).transpose(0, 1, 3, 2).reshape(rows, -1)
        return m.reshape(rows, NKV * 2, 2, HD // 2, 2).transpose(0, 1, 4, 2, 3).reshape(rows, -1)

    def by_step(*parts):
        w = np.concatenate(parts, axis=2)
        rows = w.shape[1]
        return w.reshape(NKV, rows, STEPS_G, -1).transpose(0, 2, 1, 3).reshape(TILES, rows, -1)

    codes = np.concatenate([
        by_step(cols(split_dims(i["L0_attn_q_codes"], 32))),
        by_step(cols(split_dims(i["L0_attn_k_codes"], NKV)), cols(i["L0_attn_v_codes"]),
                i["L0_attn_o_codes"].reshape(NKV, RF, P, D).transpose(0, 2, 1, 3).reshape(NKV, P, RF * D))], axis=2)

    def srow(s):
        n = s.shape[1] // NKV
        return s.reshape(KT, NKV, n).transpose(1, 0, 2).reshape(NKV, 1, KT * n)

    scales = by_step(srow(split_dims(i["L0_attn_k_scales"], NKV)),
                     srow(i["L0_attn_v_scales"]), i["L0_attn_o_scales"].reshape(NKV, 1, RF * D))[:, 0]

    inv_freq = (1.0 / np.float32(10000.0) ** (np.arange(0, HD, 2, dtype=np.float32) / np.float32(HD))).astype(np.float32)
    f = np.arange(S, dtype=np.float32)[None, :] * inv_freq[:, None]
    cos, sin = np.cos(f), np.sin(f)
    t, s = np.arange(S)[:, None], np.arange(S)[None, :]
    arrays = {
        "x": i["x"].reshape(TOKENS, D),
        "conv_w": i["L0_cond_weight"].reshape(CGROUPS, CG, CG, TAPS).transpose(0, 2, 3, 1).reshape(S, TAPS, CG),
        "cond_T": i["cond_128"].T,
        "cw_T": i["L0_cond_c_weight"].T,
        "fside": i["fside_S_0"],
        "w0": i["L0_cond2_W0"], "w1": i["L0_cond2_W1"], "w2": i["L0_cond2_W2"],
        "b0": i["L0_cond2_b0"].reshape(P, 1), "b1": i["L0_cond2_b1"].reshape(P, 1), "b2": i["L0_cond2_b2"],
        "kern": i["L0_cond2_weight"].reshape(COND_K, S, S).transpose(0, 2, 1).reshape(COND_K, S * S),
        "kern_b": i["L0_cond2_bias_k"],
        "codes": codes,
        "scales": scales,
        "base_T": i["L0_ffn_base_W"].T.reshape(KT, P, D).transpose(1, 0, 2),
        "gl_T": np.concatenate([i["L0_ffn_gate_W"].T, i["L0_ffn_lora_A"].reshape(ER, D).T], axis=1)
        .reshape(KT, P, GL).transpose(1, 0, 2),
        "lb_T": i["L0_ffn_lora_B"].transpose(0, 2, 1).reshape(2, EH, D).transpose(1, 0, 2),
        "ident": np.eye(P, dtype=np.float32),
        "iota": np.arange(EXPERTS, dtype=np.float32),
        "cos2": np.concatenate([cos, cos]),
        "sin2": np.concatenate([sin, sin]),
        "cos_k": np.concatenate([cos, cos]) / np.float32(WSCALE),
        "sin_k": np.concatenate([sin, -sin]) / np.float32(WSCALE),
        "q_scales": split_dims(i["L0_attn_q_scales"], 32).reshape(KT, NKV, 2 * 2, P).transpose(3, 1, 2, 0),
        "mask": np.tile(np.where(t > s, np.float32(-1e30), np.float32(0)), (TB, 1)),
    }
    arrays = {k: np.ascontiguousarray(v) for k, v in arrays.items()}
    nc = bacc.Bacc("TRN2", target_bir_lowering=False, num_devices=1)
    aps = {k: nc.dram_tensor(f"in_{k}", v.shape, mybir.dt.from_np(v.dtype), kind="ExternalInput").ap()
           for k, v in arrays.items()}
    out = nc.dram_tensor("out", [TOKENS, D], F32, kind="ExternalOutput").ap()
    layer(nc, aps, out)
    r = run_bass_kernel_spmd(nc, [{f"in_{k}": v for k, v in arrays.items()}], core_ids=[0])
    return r.results[0]["out"].reshape(B, S, D)
```

```python
from contextlib import ExitStack

import concourse.bass as bass
from concourse import mybir

F32 = mybir.dt.float32
F16 = mybir.dt.float16
BF16 = mybir.dt.bfloat16
I32 = mybir.dt.int32
U32 = mybir.dt.uint32
ALU = mybir.AluOpType
ACT = mybir.ActivationFunctionType
AX = mybir.AxisListType

P = 128
B, S, D = 128, 32, 512
TOKENS = B * S
TILES = TOKENS // P
TB = P // S
KT = D // P
CHUNK = 512
CHUNKS = TOKENS // CHUNK
CT = CHUNK // P
NKV, RF, HD = 8, 4, 128
TAPS, PAD, CGROUPS = 9, 4, 4
CG = S // CGROUPS
XP = D + 2 * PAD
WQ = 2048
WK, WV, WO, WKVO = 0, 512, 1024, 3072
QSTEP = WQ * NKV // TILES
WSTEP = WKVO * NKV // TILES
STEPS_G = TILES // NKV
WSCALE = 256.0
FSCALE = 64.0
SM_SCALE = float(HD) ** -0.5
EXPERTS, RANK, LORA = 28, 8, 2.0
ER = EXPERTS * RANK
EH = ER // 2
GL = EXPERTS + ER
COND_K = 8
PASSES = ((0, 0), (0, 1), (1, 0))


def layer(nc, a, out):
    w_codes = nc.dram_tensor("w_codes", [P, NKV * WQ], F16, kind="Internal").ap()
    w_split = nc.dram_tensor("w_split", [P, 2, NKV * WKVO], F16, kind="Internal").ap()
    ctx_rows = nc.dram_tensor("ctx_rows", [B, S], F32, kind="Internal").ap()
    aggb_rows = nc.dram_tensor("aggb_rows", [B, S], F32, kind="Internal").ap()
    aggw_rows = nc.dram_tensor("aggw_rows", [B, S * S], F32, kind="Internal").ap()
    with ExitStack() as ctx:
        bank = [ctx.enter_context(nc.psum_tensor(f"bank{n}", [P, 512], F32)) for n in range(8)]
        x1 = ctx.enter_context(nc.sbuf_tensor("x1", [P, TILES, D], F32))
        hT = ctx.enter_context(nc.sbuf_tensor("hT", [P, KT, 2, TOKENS], F16))
        w_ctx = ExitStack()
        w_q = w_ctx.enter_context(nc.sbuf_tensor("w_q", [P, WQ], F16))
        w_g = w_ctx.enter_context(nc.sbuf_tensor("w_g", [P, 2, WKVO], F16))
        w_loaded = [ctx.enter_context(nc.semaphore(name)) for name in ("wk_loaded", "wq_loaded", "wv_loaded", "wo_loaded")]
        with ExitStack() as c1:
            conv_w = c1.enter_context(nc.sbuf_tensor("conv_w", [P, 2, TAPS, P], F16))
            x_hl = c1.enter_context(nc.sbuf_tensor("x_hl", [P, 2, 2, XP], F16))
            agg_sb = c1.enter_context(nc.sbuf_tensor("agg_sb", [P, S * S + S], F32))
            agg_stored = c1.enter_context(nc.semaphore("agg_stored"))
            x_loaded = c1.enter_context(nc.semaphore("x_loaded"))
            setup(nc, a, bank, x1, conv_w, x_hl, agg_sb, x_loaded, agg_stored, ctx_rows, aggb_rows, aggw_rows)
            conv_and_dequant(nc, a, bank, x1, hT, conv_w, x_hl, x_loaded, agg_stored, ctx_rows, w_codes, w_split, w_q, w_g, w_loaded)
        with ExitStack() as c2:
            attention(nc, c2, a, bank, x1, hT, w_codes, w_split, w_q, w_g, w_loaded, aggb_rows, aggw_rows)
        w_ctx.close()
        with ExitStack() as c3:
            mix_and_ffn(nc, c3, a, bank, x1, hT, out)


def load_head(sp, w_q, w_g, w_loaded, w_codes, w_split, g, what):
    at = {"k": WK, "v": WV, "o": WO}
    end = {"k": WV, "v": WO, "o": WKVO}
    if what == "q":
        sp.dma_start(w_q[:], w_codes[:, bass.ds(g * WQ, WQ)]).then_inc(w_loaded["kqvo".index(what)], 16)
    else:
        sp.dma_start(w_g[:, :, at[what]:end[what]],
                     w_split[:, :, bass.ds(g * WKVO + at[what], end[what] - at[what])]).then_inc(w_loaded["kqvo".index(what)], 16)


def ffn_inputs(hT):
    words = hT[:].rearrange("p k a t -> p (k a t)").bitcast(F32)
    at = 0
    places = []
    for cols in (TILES * P, TOKENS, KT * D, KT * GL, 2 * D):
        places.append(words[:, at:at + cols])
        at += cols
    mixw_f, aggb, base_f, gl_f, lb_f = places
    return (mixw_f.rearrange("p (t o) -> p t o", o=P), aggb, base_f.rearrange("p (k n) -> p k n", k=KT),
            gl_f.rearrange("p (k n) -> p k n", k=KT), lb_f[0:EH].rearrange("p (h n) -> p h n", h=2))


def load_x(sp, a, x1, x_loaded, r):
    rows = a["x"].rearrange("(t p) l -> t p l", p=P)[bass.ds(2 * r, 2)]
    sp.dma_start(x1[:, bass.ds(2 * r, 2)], rows.rearrange("t p l -> p t l")).then_inc(x_loaded, 16)


def setup(nc, a, bank, x1, conv_w, x_hl, agg_sb, x_loaded, agg_stored, ctx_rows, aggb_rows, aggw_rows):
    with ExitStack() as c:
        def sb(name, shape, dt=F32):
            return c.enter_context(nc.sbuf_tensor(name, shape, dt))

        def sem(name):
            return c.enter_context(nc.semaphore(name))

        conv_f = sb("conv_f", [P, TAPS, P])
        params = sb("params", [P, a["params"].shape[1]])
        at = 0
        parts = []
        for cols in (B, P, 1, S, S, P, P, 1, COND_K, COND_K):
            parts.append(params[:, at:at + cols])
            at += cols
        cond_T, w0, b0, cw_T, fside, w1, ident, b1, w2, b2 = parts
        kern = sb("kern", [COND_K, S * S + S])
        ctx_sb = sb("ctx_sb", [P, S])
        hid = sb("hid", [P, 2, B])
        att = sb("att", [P, COND_K])
        att_T = sb("att_T", [COND_K, B])
        stat = sb("stat", [P, 4])

        conv_zeroed = sem("conv_zeroed")
        pads_zeroed = sem("pads_zeroed")
        conv_loaded = sem("conv_loaded")
        params_loaded = sem("params_loaded")
        conv_hi = sem("conv_hi")
        conv_lo = sem("conv_lo")
        ctx_psum = sem("ctx_psum")
        ctx_added = sem("ctx_added")
        hid_psum = sem("hid_psum")
        att_max = sem("att_max")
        hid_done = sem("hid_done")
        att_psum = sem("att_psum")
        att_step = sem("att_step")
        att_exp = sem("att_exp")
        att_T_psum = sem("att_T_psum")
        att_T_done = sem("att_T_done")
        agg_psum = sem("agg_psum")
        agg_done = sem("agg_done")
        ctx_stored = sem("ctx_stored")
        block = c.enter_context(nc.Block())

        @block.sync
        def _(sp):
            sp.dma_start(params[:], a["params"]).then_inc(params_loaded, 16)
            sp.dma_start(kern[:], a["kern"]).then_inc(params_loaded, 16)
            load_x(sp, a, x1, x_loaded, 0)
            sp.wait_ge(ctx_added, 1)
            sp.dma_start(ctx_rows, ctx_sb[:]).then_inc(ctx_stored, 16)
            sp.wait_ge(agg_done, 3)
            sp.dma_start(aggw_rows, agg_sb[:, 0:S * S]).then_inc(agg_stored, 16)
            sp.dma_start(aggb_rows, agg_sb[:, S * S:]).then_inc(agg_stored, 16)
            sp.wait_ge(ctx_stored, 16)

        @block.gpsimd
        def _(pool):
            pool.memset(conv_f[:], 0.0).then_inc(conv_zeroed, 1)
            pool.memset(x_hl[:], 0.0).then_inc(pads_zeroed, 1)

        @block.scalar
        def _(act):
            act.wait_ge(conv_zeroed, 1)
            for b in range(TB):
                act.dma_start(conv_f[S * b:S * (b + 1), :, S * b:S * (b + 1)], a["conv_w"]).then_inc(conv_loaded, 16)
            act.wait_ge(conv_loaded, 16 * TB)
            act.activation(conv_w[:, 0], conv_f[:], ACT.Copy).then_inc(conv_hi, 1)
            for n, bias in enumerate((b0, b1)):
                act.wait_ge(hid_psum, n + 1)
                act.activation(hid[:, n], bank[1 + n][:, 0:B], ACT.Gelu, bias=bias[:, 0:1]).then_inc(hid_done, 1)
            act.wait_ge(att_step, 2)
            act.activation(att[:], att[:], ACT.Exp).then_inc(att_exp, 1)

        @block.tensor
        def _(pe):
            pe.wait_ge(params_loaded, 16 * 2)
            pe.matmul(bank[0][:, 0:S], cond_T, cw_T, start=True, stop=True).then_inc(ctx_psum, 1)
            pe.matmul(bank[1][:, 0:B], w0, cond_T, start=True, stop=True).then_inc(hid_psum, 1)
            pe.wait_ge(hid_done, 1)
            pe.matmul(bank[2][:, 0:B], w1, hid[:, 0], start=True, stop=True).then_inc(hid_psum, 1)
            pe.wait_ge(hid_done, 2)
            pe.matmul(bank[3][:, 0:COND_K], hid[:, 1], w2, start=True, stop=True).then_inc(att_psum, 1)
            pe.wait_ge(att_step, 5)
            pe.transpose(bank[4][0:COND_K, 0:B], att[:], ident).then_inc(att_T_psum, 1)
            pe.wait_ge(att_T_done, 1)
            for n in range(2):
                pe.matmul(bank[5 + n][:, :], att_T[:], kern[:, 512 * n:512 * (n + 1)],
                          start=True, stop=True).then_inc(agg_psum, 1)
            pe.matmul(bank[7][:, 0:S], att_T[:], kern[:, S * S:], start=True, stop=True).then_inc(agg_psum, 1)

        @block.vector
        def _(dve):
            dve.wait_ge(ctx_psum, 1)
            dve.tensor_tensor(ctx_sb[:], bank[0][:, 0:S], fside, ALU.add).then_inc(ctx_added, 1)
            dve.wait_ge(conv_hi, 1)
            dve.tensor_tensor(conv_w[:, 1], conv_f[:], conv_w[:, 0], ALU.subtract).then_inc(conv_lo, 1)
            dve.wait_ge(att_psum, 1)
            dve.tensor_tensor(att[:], bank[3][:, 0:COND_K], b2, ALU.add).then_inc(att_step, 1)
            dve.wait_ge(att_step, 1)
            dve.tensor_reduce(stat[:, 0:1], att[:], AX.X, ALU.max).then_inc(att_max, 1)
            dve.wait_ge(att_max, 1)
            dve.tensor_scalar(att[:], att[:], stat[:, 0:1], None, ALU.subtract).then_inc(att_step, 1)
            dve.wait_ge(att_exp, 1)
            dve.reduce_sum(stat[:, 1:2], att[:], AX.X).then_inc(att_step, 1)
            dve.wait_ge(att_step, 3)
            dve.reciprocal(stat[:, 2:3], stat[:, 1:2]).then_inc(att_step, 1)
            dve.wait_ge(att_step, 4)
            dve.tensor_scalar(att[:], att[:], stat[:, 2:3], None, ALU.mult).then_inc(att_step, 1)
            dve.wait_ge(att_T_psum, 1)
            dve.tensor_copy(att_T[:], bank[4][0:COND_K, 0:B]).then_inc(att_T_done, 1)
            for n in range(2):
                dve.wait_ge(agg_psum, n + 1)
                dve.tensor_copy(agg_sb[:, 512 * n:512 * (n + 1)], bank[5 + n][:, :]).then_inc(agg_done, 1)
            dve.wait_ge(agg_psum, 3)
            dve.tensor_copy(agg_sb[:, S * S:], bank[7][:, 0:S]).then_inc(agg_done, 1)


def conv_and_dequant(nc, a, bank, x1, hT, conv_w, x_hl, x_loaded, agg_stored, ctx_rows, w_codes, w_split, w_q, w_g, w_loaded):
    with ExitStack() as c:
        def sb(name, shape, dt=F32):
            return c.enter_context(nc.sbuf_tensor(name, shape, dt))

        def sem(name):
            return c.enter_context(nc.semaphore(name))

        ctx_bc = sb("ctx_bc", [P, TOKENS])
        h_f = sb("h_f", [P, 2, KT, P])
        codes = sb("codes", [P, 2, QSTEP + WSTEP], I32)
        w_f = sb("w_f", [P, 2, WSTEP])
        wq16 = sb("wq16", [P, 2, QSTEP], F16)
        w_hl = sb("w_hl", [P, 2, 2, WSTEP], F16)

        ctx_loaded = sem("ctx_loaded")
        codes_loaded = [sem(f"codes_loaded{n}") for n in range(2)]
        w_stored = [sem(f"w_stored{n}") for n in range(2)]
        x_hi = sem("x_hi")
        x_lo = sem("x_lo")
        conv_psum = sem("conv_psum")
        h_added = sem("h_added")
        h_hi = sem("h_hi")
        h_lo = sem("h_lo")
        w_dequant = sem("w_dequant")
        w_hi = sem("w_hi")
        w_lo = sem("w_lo")
        block = c.enter_context(nc.Block())
        ROUNDS = TILES // 2

        def x_cols(n):
            return x_hl[:, n, :, PAD:PAD + D]

        @block.sync
        def _(sp):
            def load(t, n):
                sp.dma_start(codes[:, n], a["codes"][bass.ds(t, 1)].rearrange("t p n -> p (t n)")).then_inc(codes_loaded[n], 16)
                sp.dma_start(w_f[:, n], a["scales"][bass.ds(t, 1)].rearrange("t n -> (t n)")
                             .partition_broadcast(P)).then_inc(codes_loaded[n], 16)

            def store(t, n):
                sp.wait_ge(w_lo, t + 1)
                sp.dma_start(w_codes[:, bass.ds(t * QSTEP, QSTEP)], wq16[:, n]).then_inc(w_stored[n], 16)
                sp.dma_start(w_split[:, :, bass.ds(t * WSTEP, WSTEP)], w_hl[:, n]).then_inc(w_stored[n], 16)

            for n in range(2):
                load(n, n)
            sp.dma_start(ctx_bc[:], ctx_rows.rearrange("b s -> (b s)").partition_broadcast(P)).then_inc(ctx_loaded, 16)
            with sp.Fori(0, ROUNDS - 1) as r:
                sp.wait_ge(x_hi, 2 * r + 1)
                load_x(sp, a, x1, x_loaded, r + 1)
                for n in range(2):
                    store(2 * r + n, n)
                    load(2 * r + n + 2, n)
            for n in range(2):
                sp.wait_ge(w_stored[n], 32 * STEPS_G // 2)
            for what in "kqvo":
                load_head(sp, w_q, w_g, w_loaded, w_codes, w_split, 0, what)
            for n in range(2):
                store(TILES - 2 + n, n)
            for n in range(2):
                sp.wait_ge(w_stored[n], 32 * ROUNDS)
            sp.wait_ge(agg_stored, 32)

        @block.scalar
        def _(act):
            def split_x(t, r, n):
                act.wait_ge(x_loaded, 16 * (r + 1))
                act.activation(x_hl[:, n, 0, PAD:PAD + D], x1[:, bass.ds(t, 1)].rearrange("p t l -> p (t l)"),
                               ACT.Copy).then_inc(x_hi, 1)

            def rest(t, r, n, first):
                act.wait_ge(w_dequant, t + 1)
                act.activation(w_hl[:, n, 0], w_f[:, n], ACT.Copy, scale=WSCALE).then_inc(w_hi, 1)
                act.wait_ge(h_added, t + 1)
                act.activation(hT[:, :, 0, bass.ds(t * P, P)], h_f[:, n], ACT.Copy).then_inc(h_hi, 1)

            split_x(0, 0, 0)
            split_x(1, 0, 1)
            for n in range(2):
                rest(n, 0, n, True)
                split_x(n + 2, 1, n)
            with act.Fori(1, ROUNDS - 1) as r:
                for n in range(2):
                    rest(2 * r + n, r, n, False)
                    split_x(2 * r + n + 2, r + 1, n)
            for n in range(2):
                rest(TILES - 2 + n, ROUNDS - 1, n, False)

        @block.gpsimd
        def _(pool):
            def split_x(t, n):
                pool.wait_ge(x_hi, t + 1)
                pool.tensor_tensor(x_hl[:, n, 1, PAD:PAD + D], x1[:, bass.ds(t, 1)].rearrange("p t l -> p (t l)"),
                                   x_hl[:, n, 0, PAD:PAD + D], ALU.subtract).then_inc(x_lo, 1)

            def split_h(t, n):
                pool.wait_ge(h_hi, t + 1)
                pool.tensor_tensor(hT[:, :, 1, bass.ds(t * P, P)], h_f[:, n], hT[:, :, 0, bass.ds(t * P, P)],
                                   ALU.subtract).then_inc(h_lo, 1)

            for n in range(2):
                split_x(n, n)
            with pool.Fori(0, ROUNDS - 1) as r:
                for n in range(2):
                    split_h(2 * r + n, n)
                    split_x(2 * r + n + 2, n)
            for n in range(2):
                split_h(TILES - 2 + n, n)

        @block.vector
        def _(dve):
            def work(t, r, n, first):
                dve.wait_ge(codes_loaded[n], 32 * (r + 1))
                if not first:
                    dve.wait_ge(w_stored[n], 32 * r)
                dve.scalar_tensor_tensor(out=w_f[:, n], in0=codes[:, n, QSTEP:], scalar=-8.0, in1=w_f[:, n],
                                         op0=ALU.add, op1=ALU.mult).then_inc(w_dequant, 1)
                dve.tensor_scalar(wq16[:, n], codes[:, n, 0:QSTEP], -8.0, None, ALU.add)
                dve.wait_ge(w_hi, t + 1)
                dve.scalar_tensor_tensor(out=w_hl[:, n, 1], in0=w_f[:, n], scalar=WSCALE, in1=w_hl[:, n, 0],
                                         op0=ALU.mult, op1=ALU.subtract).then_inc(w_lo, 1)
                dve.wait_ge(conv_psum, t + 1)
                if not first:
                    dve.wait_ge(h_lo, t - 1)
                dve.tensor_tensor(h_f[:, n], bank[n][:].rearrange("p (k t) -> p k t", k=KT),
                                  ctx_bc[:, bass.ds(t * P, P)].unsqueeze(1).broadcast_to([P, KT, P]),
                                  ALU.add).then_inc(h_added, 1)

            dve.wait_ge(ctx_loaded, 16)
            for n in range(2):
                work(n, 0, n, True)
            with dve.Fori(1, ROUNDS) as r:
                for n in range(2):
                    work(2 * r + n, r, n, False)

        @block.tensor
        def _(pe):
            def conv(t, n, first):
                pe.wait_ge(x_lo, t + 1)
                if not first:
                    pe.wait_ge(h_added, t - 1)
                for k in range(KT):
                    for tap in range(TAPS):
                        for xp, wp in PASSES:
                            mm = pe.matmul(bank[n][:, k * P:(k + 1) * P], x_hl[:, n, xp, k * P + tap:k * P + tap + P],
                                           conv_w[:, wp, tap], start=tap == 0 and (xp, wp) == PASSES[0],
                                           stop=tap == TAPS - 1 and (xp, wp) == PASSES[-1])
                mm.then_inc(conv_psum, 1)

            for n in range(2):
                conv(n, n, True)
            with pe.Fori(1, ROUNDS) as r:
                for n in range(2):
                    conv(2 * r + n, n, False)


def attention(nc, c, a, bank, x1, hT, w_codes, w_split, w_q, w_g, w_loaded, aggb_rows, aggw_rows):
    def sb(name, shape, dt=F32):
        return c.enter_context(nc.sbuf_tensor(name, shape, dt))

    def sem(name):
        return c.enter_context(nc.semaphore(name))

    STEPS = NKV * CHUNKS
    q_scales = sb("q_scales", [P, NKV, 4, KT])
    q_sum = sb("q_sum", [P, 2, 2, CHUNK])
    q_hl = sb("q_hl", [P, 2, RF, CHUNK], F16)
    k_hl = sb("k_hl", [P, 2, CHUNK], F16)
    v_hl = sb("v_hl", [P, 2, CT, HD], F16)
    o_hl = sb("o_hl", [P, 2, CT, RF, P], F16)
    pad_hl = sb("pad_hl", [P, 2 * CT * RF, TB, S], F16)
    prod = sb("prod", [P, 2, 2, CHUNK])
    y_hl = sb("y_hl", [P, 2, CHUNK], F16)
    k_prod = sb("k_prod", [P, 2, CHUNK])
    sc = sb("sc", [P, CHUNK])
    p_hl = sb("p_hl", [P, 2, CHUNK], F16)
    pT_hl = sb("pT_hl", [P, 2 * CT * RF, S], F16)
    stats = sb("stats", [P, 3, CT * RF])
    cos2 = sb("cos2", [P, S])
    sin2 = sb("sin2", [P, S])
    cos_k = sb("cos_k", [P, S])
    sin_k = sb("sin_k", [P, S])
    mask_f = sb("mask_f", [P, S])
    ident_f = sb("ident_f", [P, P])
    mask_b = sb("mask_b", [P, CT * RF, S], BF16)
    ident_b = sb("ident_b", [P, P], BF16)

    consts_loaded = sem("consts_loaded")
    consts_ready = sem("consts_ready")
    pad_zeroed = sem("pad_zeroed")
    wk_loaded, wq_loaded, wv_loaded, wo_loaded = w_loaded
    mixw_zeroed = sem("mixw_zeroed")
    ffn_loaded = sem("ffn_loaded")
    mixw_f, aggb, base_f, gl_f, lb_f = ffn_inputs(hT)
    k_psum = sem("k_psum")
    q_psum = sem("q_psum")
    q_scaled = sem("q_scaled")
    q_summed = sem("q_summed")
    q_total = sem("q_total")
    q_last_total = sem("q_last_total")
    v_psum = sem("v_psum")
    scores_psum = sem("scores_psum")
    pv_psum = sem("pv_psum")
    o_psum = sem("o_psum")
    k_products = sem("k_products")
    k_rotated = sem("k_rotated")
    k_hi = sem("k_hi")
    k_ready = sem("k_ready")
    q_products = sem("q_products")
    q_rotated = sem("q_rotated")
    q_hi = sem("q_hi")
    q_lo = sem("q_lo")
    q_last_lo = sem("q_last_lo")
    q_moved = sem("q_moved")
    q_ready = sem("q_ready")
    v_hi = sem("v_hi")
    v_ready = sem("v_ready")
    sc_read = sem("sc_read")
    max_done = sem("max_done")
    shifted = sem("shifted")
    exp_done = sem("exp_done")
    sum_done = sem("sum_done")
    inv_done = sem("inv_done")
    probs = sem("probs")
    probs_hi = sem("probs_hi")
    probs_lo = sem("probs_lo")
    probs_T = sem("probs_T")
    probs_padded = sem("probs_padded")
    out_hi = sem("out_hi")
    out_ready = sem("out_ready")
    x1_added = sem("x1_added")
    block = c.enter_context(nc.Block())

    def w_cols(part, col, n):
        return w_g[:, part, col:col + n]

    def head_of(n):
        return n // CHUNKS if isinstance(n, int) else n >> 3

    def q_scale(n, tile, kt):
        head = head_of(n) if isinstance(n, int) else head_of(n) & (NKV - 1)
        return q_scales[:, bass.ds(head, 1), tile, kt]

    def table(t, parts=slice(0, P)):
        n = parts.stop - parts.start
        return t[parts, :].unsqueeze(1).broadcast_to([n, CHUNK // S, S])

    def by_s(ap):
        return ap.rearrange("p (b s) -> p b s", s=S)

    @block.sync
    def _(sp):
        for dst, src in ((cos2, a["cos2"]), (sin2, a["sin2"]), (cos_k, a["cos_k"]), (sin_k, a["sin_k"]),
                         (q_scales, a["q_scales"]), (mask_f, a["mask"]), (ident_f, a["ident"])):
            sp.dma_start(dst[:], src).then_inc(consts_loaded, 16)

        def load(g, what):
            load_head(sp, w_q, w_g, w_loaded, w_codes, w_split, g, what)

        with sp.Fori(1, NKV) as g:
            sp.wait_ge(q_psum, 4 * KT * CHUNKS * g)
            load(g, "q")
            sp.wait_ge(k_psum, CHUNKS * g)
            load(g, "k")
            sp.wait_ge(v_psum, CHUNKS * g)
            load(g, "v")
            sp.wait_ge(o_psum, CT * CHUNKS * g)
            load(g, "o")
        sp.wait_ge(mixw_zeroed, 1)
        for b in range(TB):
            sp.dma_start(mixw_f[b * S:(b + 1) * S, :, b * S:(b + 1) * S],
                         aggw_rows.rearrange("(t b) (i o) -> b i t o", b=TB, i=S)[b]).then_inc(ffn_loaded, 16)
        for dst, src in ((base_f, a["base_T"]), (gl_f, a["gl_T"]), (lb_f, a["lb_T"]),
                         (aggb, aggb_rows.rearrange("b s -> (b s)").partition_broadcast(P))):
            sp.dma_start(dst, src).then_inc(ffn_loaded, 16)
        sp.wait_ge(ffn_loaded, 16 * (TB + 4))

    @block.tensor
    def _(pe):
        def tok(n):
            return n % CHUNKS * CHUNK if isinstance(n, int) else (n & (CHUNKS - 1)) * CHUNK

        def project_k(n):
            t0 = tok(n)
            pe.wait_ge(wk_loaded, 16 * (head_of(n) + 1))
            i = 0
            for kt in range(KT):
                for wp, hp in PASSES:
                    mm = pe.matmul(bank[4][:], w_cols(wp, WK + kt * HD, HD), hT[:, kt, hp, bass.ds(t0, CHUNK)],
                                   start=i == 0, stop=i == 3 * KT - 1)
                    i += 1
            mm.then_inc(k_psum, 1)

        def project_q(n, pair):
            t0 = tok(n)
            if pair == 0:
                pe.wait_ge(wq_loaded, 16 * (head_of(n) + 1))
            for tile in (2 * pair, 2 * pair + 1):
                for kt in range(KT):
                    if tile:
                        pe.wait_ge(q_scaled if kt < 2 else q_summed, 8 * n + 2 * tile - 1 + kt % 2)
                    for hp in range(2):
                        mm = pe.matmul(bank[kt][:], w_q[:, kt * 512 + tile * P:kt * 512 + (tile + 1) * P],
                                       hT[:, kt, hp, bass.ds(t0, CHUNK)], start=hp == 0, stop=hp == 1)
                    mm.then_inc(q_psum, 1)

        def project_v(n):
            t0 = tok(n)
            pe.wait_ge(wv_loaded, 16 * (head_of(n) + 1))
            for j in range(CT):
                i = 0
                for kt in range(KT):
                    for hp, wp in PASSES:
                        mm = pe.matmul(bank[5][:, j * HD:(j + 1) * HD], hT[:, kt, hp, bass.ds(t0 + j * P, P)],
                                       w_cols(wp, WV + kt * HD, HD), start=i == 0, stop=i == 3 * KT - 1)
                        i += 1
                        if j < CT - 1 or i < 3 * KT:
                            yield
            mm.then_inc(v_psum, 1)
            yield

        def scores(i):
            pe.wait_ge(k_ready, i + 1)
            pe.wait_ge(q_ready, 2 * i + 2)
            pe.matmul(bank[6][:], ident_b[:], mask_b[:].rearrange("p n s -> p (n s)"), start=True, stop=False,
                      skip_group_check=True)
            for j in range(CT):
                for kp, qp in PASSES:
                    for b in range(TB):
                        t = j * P + b * S
                        mm = pe.matmul(bank[6][b * S:(b + 1) * S, j * P:(j + 1) * P], k_hl[:, kp, t:t + S],
                                       q_hl[:, qp, :, t:t + S], start=False, stop=(kp, qp) == PASSES[-1] and j == CT - 1,
                                       skip_group_check=True)
            mm.then_inc(scores_psum, 1)

        def values(i, n=None, v=None):
            pe.wait_ge(probs_padded, i + 1)
            pe.wait_ge(v_ready, i + 1)
            if n is not None:
                pe.wait_ge(q_scaled, 8 * n + 8)
                pe.wait_ge(q_summed, 8 * n + 8)
            for j in range(CT):
                for m, (vp, pp) in enumerate(PASSES):
                    mm = pe.matmul(bank[j][:], v_hl[:, vp, j],
                                   pad_hl[:, (pp * CT + j) * RF:(pp * CT + j + 1) * RF].rearrange("p n b s -> p (n b s)"),
                                   start=m == 0, stop=m == 2)
                    if m == 2:
                        mm.then_inc(pv_psum, 1)
                    if v is not None:
                        for _ in range(KT):
                            next(v)

        def output(i, tiles, busy=True):
            if tiles[0] == 0:
                pe.wait_ge(wo_loaded, 16 * (head_of(i) + 1))
            for j in tiles:
                pe.wait_ge(out_ready, CT * i + j + 1)
                if j == 0 and busy:
                    pe.wait_ge(v_ready, i + 2)
                if j >= 2:
                    pe.wait_ge(x1_added, CT * i + j - 1)
                n = 0
                for h in range(RF):
                    for op, wp in PASSES:
                        mm = pe.matmul(bank[5 + j % 2 * 2][:], o_hl[:, op, j, h], w_o(wp, h), start=n == 0, stop=n == 3 * RF - 1)
                        n += 1
                mm.then_inc(o_psum, 1)

        def w_o(part, h):
            return w_cols(part, WO + h * D, D)

        project_k(0)
        project_q(0, 0)
        for _ in project_v(0):
            pass
        project_q(0, 1)
        pe.wait_ge(k_ready, 1)
        project_k(1)
        pe.wait_ge(consts_ready, 2)
        scores(0)
        project_q(1, 0)
        project_q(1, 1)
        values(0, 1, project_v(1))
        with pe.Fori(1, STEPS - 1) as i:
            scores(i)
            project_k(i + 1)
            pe.wait_ge(out_ready, CT * i)
            project_q(i + 1, 0)
            output(i - 1, (0, 1))
            project_q(i + 1, 1)
            output(i - 1, (2, 3))
            pe.wait_ge(x1_added, CT * i - 1)
            values(i, i + 1, project_v(i + 1))
            pe.wait_ge(x1_added, CT * i)
        scores(STEPS - 1)
        output(STEPS - 2, range(CT))
        values(STEPS - 1)
        pe.wait_ge(x1_added, CT * (STEPS - 1))
        output(STEPS - 1, range(CT), busy=False)

    @block.vector
    def _(dve):
        def rotate_k(n):
            dve.wait_ge(k_psum, n + 1)
            dve.tensor_tensor(by_s(k_prod[:, 0]), by_s(bank[4][:]), table(cos_k), ALU.mult)
            for h in range(2):
                src = slice(64 * (1 - h), 64 * (2 - h))
                ins = dve.tensor_tensor(by_s(k_prod[64 * h:64 * (h + 1), 1]), by_s(bank[4][src, :]), table(sin_k, src), ALU.mult)
            ins.then_inc(k_products, 1)

        def sum_q(n, tile):
            for kt in range(2, KT):
                half = q_sum[:, tile % 2, kt - 2]
                dve.wait_ge(q_psum, 4 * KT * n + KT * tile + kt + 1)
                dve.wait_ge(q_scaled, 8 * n + 2 * tile + kt - 1)
                dve.scalar_tensor_tensor(out=half, in0=bank[kt][:], scalar=q_scale(n, tile, kt), in1=half,
                                         op0=ALU.mult, op1=ALU.add).then_inc(q_summed, 1)

        def total_last(n):
            dve.wait_ge(q_summed, 8 * n + 8)
            dve.tensor_tensor(q_sum[:, 1, 0], q_sum[:, 1, 0], q_sum[:, 1, 1], ALU.add).then_inc(q_last_total, 1)

        def rotate_q(n, stage):
            eo = stage % 2
            if stage == 0:
                dve.wait_ge(q_total, 3 * n + 2)
            if stage == 2:
                dve.wait_ge(q_total, 3 * n + 3)
                dve.wait_ge(q_last_total, n + 1)
            if stage >= 2:
                dve.wait_ge(q_lo, 3 * n + stage - 1)
            dve.tensor_tensor(by_s(prod[:, eo, 0]), by_s(q_sum[:, eo, 0]), table(cos2), ALU.mult)
            dve.tensor_tensor(by_s(prod[:, eo, 1]), by_s(q_sum[:, 1 - eo, 0]), table(sin2), ALU.mult).then_inc(q_products, 1)

        def q_low_last(n):
            dve.wait_ge(q_hi, 4 * n + 4)
            dve.tensor_tensor(y_hl[:, 1], prod[:, 1, 0], y_hl[:, 0], ALU.subtract).then_inc(q_last_lo, 1)

        def gather_q(n, pair):
            even, odd = 2 * pair, 2 * pair + 1
            if pair == 0:
                dve.wait_ge(q_lo, 3 * n + 2)
            else:
                dve.wait_ge(q_lo, 3 * n + 3)
                dve.wait_ge(q_last_lo, n + 1)
            dve.tensor_copy(q_hl[0:64, :, odd], q_hl[64:128, :, even]).then_inc(q_moved, 1)
            dve.tensor_copy(q_hl[64:128, :, odd], y_hl[64:128])
            dve.wait_ge(q_moved, 2 * n + pair + 1)
            dve.tensor_copy(q_hl[64:128, :, even], y_hl[0:64]).then_inc(q_ready, 1)

        def finish_v(n):
            dve.wait_ge(v_hi, n + 1)
            dve.scalar_tensor_tensor(out=v_hl[:, 1].rearrange("p j d -> p (j d)"), in0=bank[5][:], scalar=1 / WSCALE,
                                     in1=v_hl[:, 0].rearrange("p j d -> p (j d)"), op0=ALU.mult,
                                     op1=ALU.subtract).then_inc(v_ready, 1)

        def softmax_exp(i):
            dve.wait_ge(scores_psum, i + 1)
            dve.transpose(sc[:], bank[6][:]).then_inc(sc_read, 1)
            dve.wait_ge(sc_read, i + 1)
            dve.tensor_reduce(stats[:, 0], by_s(sc[:]), AX.X, ALU.max).then_inc(max_done, 1)
            dve.wait_ge(max_done, i + 1)
            dve.tensor_tensor(by_s(sc[:]), by_s(sc[:]), stats[:, 0].unsqueeze(2).broadcast_to([P, CT * RF, S]),
                              ALU.subtract).then_inc(shifted, 1)

        def softmax_norm(i):
            dve.wait_ge(exp_done, i + 1)
            dve.reduce_sum(stats[:, 1], by_s(sc[:]), AX.X).then_inc(sum_done, 1)
            dve.wait_ge(sum_done, i + 1)
            dve.reciprocal(stats[:, 2], stats[:, 1]).then_inc(inv_done, 1)
            dve.wait_ge(inv_done, i + 1)
            dve.tensor_tensor(by_s(sc[:]), by_s(sc[:]), stats[:, 2].unsqueeze(2).broadcast_to([P, CT * RF, S]),
                              ALU.mult).then_inc(probs, 1)

        def softmax_T(i):
            dve.wait_ge(probs_lo, i + 1)
            dve.transpose(pT_hl[:].rearrange("p n s -> p (n s)"), p_hl[:].rearrange("p h n -> p (h n)")).then_inc(probs_T, 1)

        def finish_out(i, tiles):
            for j in tiles:
                dve.wait_ge(out_hi, CT * i + j + 1)
                dve.tensor_tensor(o_hl[:, 1, j].rearrange("p h t -> p (h t)"), bank[j][:],
                                  o_hl[:, 0, j].rearrange("p h t -> p (h t)"), ALU.subtract).then_inc(out_ready, 1)

        def add_out(i, j):
            tile = (i % CHUNKS if isinstance(i, int) else i & (CHUNKS - 1)) * CT + j
            dst = x1[:, bass.ds(tile, 1)].rearrange("p t l -> p (t l)")
            dve.wait_ge(o_psum, CT * i + j + 1)
            dve.scalar_tensor_tensor(out=dst, in0=bank[5 + j % 2 * 2][:], scalar=1 / WSCALE, in1=dst,
                                     op0=ALU.mult, op1=ALU.add).then_inc(x1_added, 1)

        dve.wait_ge(consts_loaded, 16 * 7)
        dve.tensor_copy(mask_b[:], mask_f[:].unsqueeze(1).broadcast_to([P, CT * RF, S])).then_inc(consts_ready, 1)
        dve.tensor_copy(ident_b[:], ident_f[:]).then_inc(consts_ready, 1)
        def body(i, n, prior):
            def add(j):
                if prior is not None:
                    add_out(prior, j)

            softmax_exp(i)
            rotate_k(n)
            sum_q(n, 0)
            sum_q(n, 1)
            softmax_norm(i)
            rotate_q(n, 0)
            rotate_q(n, 1)
            softmax_T(i)
            sum_q(n, 2)
            add(0)
            sum_q(n, 3)
            add(1)
            gather_q(n, 0)
            total_last(n)
            add(2)
            rotate_q(n, 2)
            rotate_q(n, 3)
            add(3)
            finish_out(i, (0,))
            q_low_last(n)
            gather_q(n, 1)
            finish_out(i, (1, 2, 3))
            finish_v(n)

        rotate_k(0)
        sum_q(0, 0)
        sum_q(0, 1)
        rotate_q(0, 0)
        rotate_q(0, 1)
        sum_q(0, 2)
        sum_q(0, 3)
        total_last(0)
        gather_q(0, 0)
        rotate_q(0, 2)
        rotate_q(0, 3)
        q_low_last(0)
        gather_q(0, 1)
        finish_v(0)
        body(0, 1, None)
        with dve.Fori(1, STEPS - 1) as i:
            body(i, i + 1, i - 1)
        softmax_exp(STEPS - 1)
        softmax_norm(STEPS - 1)
        softmax_T(STEPS - 1)
        for j in range(CT):
            add_out(STEPS - 2, j)
        finish_out(STEPS - 1, range(CT))
        for j in range(CT):
            add_out(STEPS - 1, j)

    @block.gpsimd
    def _(pool):
        def rotate_k(n):
            pool.wait_ge(k_products, n + 1)
            pool.tensor_tensor(k_prod[:, 0], k_prod[:, 0], k_prod[:, 1], ALU.add).then_inc(k_rotated, 1)

        def finish_k(n):
            pool.wait_ge(k_hi, n + 1)
            pool.tensor_tensor(k_hl[:, 1], k_prod[:, 0], k_hl[:, 0], ALU.subtract).then_inc(k_ready, 1)

        def total_q(n, tile):
            pool.wait_ge(q_summed, 8 * n + 2 * tile + 2)
            pool.tensor_tensor(q_sum[:, tile % 2, 0], q_sum[:, tile % 2, 0], q_sum[:, tile % 2, 1],
                               ALU.add).then_inc(q_total, 1)

        def rotate_q(n, pair):
            for eo in range(2):
                pool.wait_ge(q_products, 4 * n + 2 * pair + eo + 1)
                pool.tensor_tensor(prod[:, eo, 0], prod[:, eo, 0], prod[:, eo, 1],
                                   ALU.add if eo else ALU.subtract).then_inc(q_rotated, 1)
            for eo in range(2 - pair):
                dst = y_hl if eo else q_hl[:, :, 2 * pair]
                pool.wait_ge(q_hi, 4 * n + 2 * pair + eo + 1)
                pool.tensor_tensor(dst[:, 1], prod[:, eo, 0], dst[:, 0], ALU.subtract).then_inc(q_lo, 1)

        def probs_low(i):
            pool.wait_ge(probs_hi, i + 1)
            pool.tensor_tensor(p_hl[:, 1], sc[:], p_hl[:, 0], ALU.subtract).then_inc(probs_lo, 1)

        pool.memset(pad_hl[:], 0.0).then_inc(pad_zeroed, 1)
        rotate_k(0)
        total_q(0, 0)
        total_q(0, 1)
        finish_k(0)
        rotate_q(0, 0)
        total_q(0, 2)
        rotate_q(0, 1)
        with pool.Fori(0, STEPS - 1) as i:
            rotate_k(i + 1)
            total_q(i + 1, 0)
            finish_k(i + 1)
            total_q(i + 1, 1)
            probs_low(i)
            rotate_q(i + 1, 0)
            total_q(i + 1, 2)
            rotate_q(i + 1, 1)
        pool.wait_ge(v_psum, STEPS)
        pool.memset(mixw_f, 0.0).then_inc(mixw_zeroed, 1)
        probs_low(STEPS - 1)

    @block.scalar
    def _(act):
        def exp(i):
            act.wait_ge(shifted, i + 1)
            act.activation(sc[:], sc[:], ACT.Exp, scale=SM_SCALE).then_inc(exp_done, 1)

        def k_high(n):
            act.wait_ge(k_rotated, n + 1)
            act.activation(k_hl[:, 0], k_prod[:, 0], ACT.Copy).then_inc(k_hi, 1)

        def probs_high(i):
            act.wait_ge(probs, i + 1)
            act.activation(p_hl[:, 0], sc[:], ACT.Copy).then_inc(probs_hi, 1)

        def scale_q(n, tile):
            if tile >= 2:
                act.wait_ge(q_products, 4 * n + 2)
            for kt in range(2):
                act.wait_ge(q_psum, 4 * KT * n + KT * tile + kt + 1)
                act.activation(q_sum[:, tile % 2, kt], bank[kt][:], ACT.Copy, scale=q_scale(n, tile, kt)).then_inc(q_scaled, 1)

        def q_high(n, stage):
            act.wait_ge(q_rotated, 4 * n + stage + 1)
            if stage == 3:
                act.wait_ge(q_ready, 2 * n + 1)
            dst = y_hl if stage % 2 else q_hl[:, :, stage]
            act.activation(dst[:, 0], prod[:, stage % 2, 0], ACT.Copy).then_inc(q_hi, 1)

        def pad(i):
            act.wait_ge(probs_T, i + 1)
            for b in range(TB):
                ins = act.activation(pad_hl[b * S:(b + 1) * S, :, b], pT_hl[b * S:(b + 1) * S], ACT.Copy)
            ins.then_inc(probs_padded, 1)

        def v_high(n):
            act.wait_ge(v_psum, n + 1)
            act.activation(v_hl[:, 0].rearrange("p j d -> p (j d)"), bank[5][:], ACT.Copy, scale=1 / WSCALE).then_inc(v_hi, 1)

        def out_high(i, j):
            act.wait_ge(pv_psum, CT * i + j + 1)
            act.activation(o_hl[:, 0, j].rearrange("p h t -> p (h t)"), bank[j][:], ACT.Copy).then_inc(out_hi, 1)

        def body(i, n):
            exp(i)
            scale_q(n, 0)
            scale_q(n, 1)
            k_high(n)
            probs_high(i)
            scale_q(n, 2)
            q_high(n, 0)
            scale_q(n, 3)
            q_high(n, 1)
            pad(i)
            out_high(i, 0)
            q_high(n, 2)
            q_high(n, 3)
            out_high(i, 1)
            out_high(i, 2)
            out_high(i, 3)
            v_high(n)

        act.wait_ge(consts_loaded, 16 * 7)
        scale_q(0, 0)
        scale_q(0, 1)
        k_high(0)
        q_high(0, 0)
        scale_q(0, 2)
        scale_q(0, 3)
        q_high(0, 1)
        q_high(0, 2)
        q_high(0, 3)
        v_high(0)
        act.wait_ge(pad_zeroed, 1)
        body(0, 1)
        with act.Fori(1, STEPS - 1) as i:
            body(i, i + 1)
        exp(STEPS - 1)
        probs_high(STEPS - 1)
        pad(STEPS - 1)
        for j in range(CT):
            out_high(STEPS - 1, j)


def mix_and_ffn(nc, c, a, bank, x1, hT, out):
    def sb(name, shape, dt=F32):
        return c.enter_context(nc.sbuf_tensor(name, shape, dt))

    def sem(name):
        return c.enter_context(nc.semaphore(name))

    mixw_f, aggb, base_f, gl_f, lb_f = ffn_inputs(hT)
    mixw = sb("mixw", [P, 2, TILES, P], F16)
    base = sb("base", [P, 2, KT, D], F16)
    gl = sb("gl", [P, 2, KT, GL], F16)
    lb = sb("lb", [EH, 2, 2, D], F16)
    ident = sb("ident_m", [P, P])
    iota = sb("iota", [P, EXPERTS])
    x_hl = sb("xm_hl", [P, 2, 2, D], F16)
    y_f = sb("y_f", [P, 2, D])
    y_hl = sb("ym_hl", [P, 2, 2, D], F16)
    logits = sb("logits", [P, 2, EXPERTS])
    top = sb("top", [P, 2, 8])
    top_at = sb("top_at", [P, 2, 8], U32)
    topv = sb("topv", [P, 2, 8])
    gates = sb("gates", [P, 2, 2, EXPERTS])
    lora = sb("lora", [P, 2, ER])
    loraT = sb("loraT", [EH, 2, 2, 2, P], F16)
    res = sb("res", [P, 2, D])

    w_loaded = sem("w_loaded")
    w_his = sem("w_his")
    w_ready = sem("w_ready")
    xs_hi = sem("xs_hi")
    xs_ready = sem("xs_ready")
    y_psum = sem("y_psum")
    y_added = sem("y_added")
    y_hi = sem("y_hi")
    y_ready = sem("y_ready")
    gl_psum = sem("gl_psum")
    base_psum = sem("base_psum")
    gate_step = sem("gate_step")
    gate_exp = sem("gate_exp")
    lora_gated = sem("lora_gated")
    loraT_psum = sem("loraT_psum")
    loraT_hi = sem("loraT_hi")
    loraT_ready = sem("loraT_ready")
    ffn_psum = sem("ffn_psum")
    res_done = sem("res_done")
    out_stored = [sem(f"out_stored{n}") for n in range(2)]
    block = c.enter_context(nc.Block())
    ROUNDS = TILES // 2
    GATE_STEPS = 9
    out_rows = out.rearrange("(t p) l -> t p l", p=P)

    def tile_of(t):
        return x1[:, bass.ds(t, 1)].rearrange("p t l -> p (t l)")

    FIRST = TILES // 8
    splits = ((mixw[:, :, 0:FIRST], mixw_f[:, 0:FIRST]), (gl[:], gl_f), (base[:], base_f), (lb[:], lb_f),
              (mixw[:, :, FIRST:], mixw_f[:, FIRST:]))
    MIXW_SPLIT, GL_SPLIT, BASE_SPLIT, LB_SPLIT, ALL_SPLIT = range(1, 6)

    @block.sync
    def _(sp):
        for dst, src in ((ident, a["ident"]), (iota, a["iota"].partition_broadcast(P))):
            sp.dma_start(dst[:], src).then_inc(w_loaded, 16)
        with sp.Fori(0, ROUNDS) as r:
            for n in range(2):
                t = 2 * r + n
                sp.wait_ge(res_done, t + 1)
                sp.dma_start(out_rows[bass.ds(t, 1)].rearrange("t p l -> p (t l)"), res[:, n]).then_inc(out_stored[n], 16)
        for n in range(2):
            sp.wait_ge(out_stored[n], 16 * ROUNDS)

    @block.tensor
    def _(pe):
        def mix(t, n):
            pe.wait_ge(xs_ready, t + 1)
            for k in range(KT):
                for i, (xp, wp) in enumerate(PASSES):
                    mm = pe.matmul(bank[n][:, k * P:(k + 1) * P], x_hl[:, n, xp, k * P:(k + 1) * P],
                                   mixw[:, wp, bass.ds(t, 1)].rearrange("p t o -> p (t o)"), start=i == 0, stop=i == 2)
            mm.then_inc(y_psum, 1)

        def gate_lora(t, n):
            pe.wait_ge(y_ready, t + 1)
            if isinstance(t, int) and t == 0:
                pe.wait_ge(w_ready, GL_SPLIT)
            i = 0
            for k in range(KT):
                for yp, wp in PASSES:
                    mm = pe.matmul(bank[4 + n][:, 0:GL], y_hl[:, n, yp, k * P:(k + 1) * P], gl[:, wp, k],
                                   start=i == 0, stop=i == 3 * KT - 1)
                    i += 1
            mm.then_inc(gl_psum, 1)

        def base_out(t, n, first):
            if not first:
                pe.wait_ge(res_done, t - 1)
            elif n == 0:
                pe.wait_ge(w_ready, BASE_SPLIT)
            i = 0
            for k in range(KT):
                for yp, wp in PASSES:
                    pe.matmul(bank[2 + n][:], y_hl[:, n, yp, k * P:(k + 1) * P], base[:, wp, k],
                              start=i == 0, stop=False, skip_group_check=True)
                    i += 1

        def lora_transpose(t, n):
            pe.wait_ge(lora_gated, t + 1)
            for h in range(2):
                mm = pe.transpose(bank[6 + n][0:EH, h * P:(h + 1) * P], lora[:, n, h * EH:(h + 1) * EH], ident[:])
            mm.then_inc(loraT_psum, 1)

        def lora_out(t, n):
            pe.wait_ge(loraT_ready, t + 1)
            if isinstance(t, int) and t == 0:
                pe.wait_ge(w_ready, LB_SPLIT)
            for h in range(2):
                for i, (lp, wp) in enumerate(PASSES):
                    mm = pe.matmul(bank[2 + n][:], loraT[:, n, lp, h], lb[:, wp, h], start=False,
                                   stop=h == 1 and i == 2, skip_group_check=True)
            mm.then_inc(ffn_psum, 1)

        def body(t, n, first, last):
            gate_lora(t, n)
            if not last:
                mix(t + 1, 1 - n)
            if not (first and n == 0):
                lora_out(t - 1, 1 - n)
            base_out(t, n, first)
            lora_transpose(t, n)

        pe.wait_ge(w_ready, MIXW_SPLIT)
        mix(0, 0)
        pe.wait_ge(w_loaded, 16 * 2)
        for n in range(2):
            body(n, n, True, False)
        pe.wait_ge(w_ready, ALL_SPLIT)
        with pe.Fori(1, ROUNDS - 1) as r:
            for n in range(2):
                body(2 * r + n, n, False, False)
        for n in range(2):
            body(TILES - 2 + n, n, False, n == 1)
        lora_out(TILES - 1, 1)

    @block.scalar
    def _(act):
        def x_high(t, n):
            act.activation(x_hl[:, n, 0], tile_of(t), ACT.Copy).then_inc(xs_hi, 1)

        def y_high(t, n):
            act.wait_ge(y_added, t + 1)
            act.activation(y_hl[:, n, 0], y_f[:, n], ACT.Copy).then_inc(y_hi, 1)

        def exp(t, n):
            act.wait_ge(gate_step, GATE_STEPS * t + 3)
            act.activation(topv[:, n, 3:4], topv[:, n, 2:3], ACT.Exp).then_inc(gate_exp, 1)

        def lora_high(t, n):
            act.wait_ge(loraT_psum, t + 1)
            act.activation(loraT[:, n, 0], bank[6 + n][0:EH, 0:2 * P].rearrange("p (h t) -> p h t", h=2),
                           ACT.Copy).then_inc(loraT_hi, 1)

        def split_high(k):
            dst, src = splits[k]
            act.activation(dst[:, 0], src, ACT.Copy, scale=FSCALE).then_inc(w_his, 1)

        split_high(0)
        x_high(0, 0)
        x_high(1, 1)
        for k in range(1, len(splits)):
            split_high(k)
        y_high(0, 0)
        with act.Fori(0, ROUNDS - 1) as r:
            for n in range(2):
                x_high(2 * r + n + 2, n)
                exp(2 * r + n, n)
                y_high(2 * r + n + 1, 1 - n)
                lora_high(2 * r + n, n)
        exp(TILES - 2, 0)
        y_high(TILES - 1, 1)
        lora_high(TILES - 2, 0)
        exp(TILES - 1, 1)
        lora_high(TILES - 1, 1)

    @block.gpsimd
    def _(pool):
        def x_low(t, n):
            pool.wait_ge(xs_hi, t + 1)
            pool.tensor_tensor(x_hl[:, n, 1], tile_of(t), x_hl[:, n, 0], ALU.subtract).then_inc(xs_ready, 1)

        def y_low(t, n):
            pool.wait_ge(y_hi, t + 1)
            pool.tensor_tensor(y_hl[:, n, 1], y_f[:, n], y_hl[:, n, 0], ALU.subtract).then_inc(y_ready, 1)

        x_low(0, 0)
        x_low(1, 1)
        y_low(0, 0)
        with pool.Fori(0, ROUNDS - 1) as r:
            for n in range(2):
                x_low(2 * r + n + 2, n)
                y_low(2 * r + n + 1, 1 - n)
        y_low(TILES - 1, 1)

    @block.vector
    def _(dve):
        def add_bias(t, n):
            dve.wait_ge(y_psum, t + 1)
            dve.scalar_tensor_tensor(out=y_f[:, n].rearrange("p (k t) -> p k t", k=KT),
                                     in0=bank[n][:].rearrange("p (k t) -> p k t", k=KT), scalar=1 / FSCALE,
                                     in1=aggb[:, bass.ds(t * P, P)].unsqueeze(1).broadcast_to([P, KT, P]),
                                     op0=ALU.mult, op1=ALU.add).then_inc(y_added, 1)

        def gate(t, n, last):
            count = [0]

            def step(ins):
                count[0] += 1
                ins.then_inc(gate_step, 1)
                dve.wait_ge(gate_step, GATE_STEPS * t + count[0])

            v = topv[:, n]
            dve.wait_ge(gl_psum, t + 1)
            step(dve.tensor_scalar(logits[:, n], bank[4 + n][:, 0:EXPERTS], 1 / FSCALE, None, ALU.mult))
            dve.memset(v[:, 7:8], 0.0)
            step(dve.max(top[:, n], logits[:, n]))
            step(dve.tensor_tensor(v[:, 2:3], top[:, n, 1:2], top[:, n, 0:1], ALU.subtract))
            dve.memset(v[:, 7:8], 0.0)
            step(dve.max_index(top_at[:, n], top[:, n], logits[:, n]))
            dve.tensor_copy(v[:, 0:2], top_at[:, n, 0:2])
            if not last:
                add_bias(t + 1, 1 - n)
            dve.wait_ge(gate_exp, t + 1)
            step(dve.tensor_scalar(v[:, 4:5], v[:, 3:4], 1.0, None, ALU.add))
            step(dve.reciprocal(v[:, 5:6], v[:, 4:5]))
            step(dve.tensor_tensor(v[:, 6:7], v[:, 3:4], v[:, 5:6], ALU.mult))
            dve.tensor_scalar(gates[:, n, 0], iota[:], v[:, 0:1], v[:, 5:6], ALU.is_equal, ALU.mult)
            step(dve.tensor_scalar(gates[:, n, 1], iota[:], v[:, 1:2], v[:, 6:7], ALU.is_equal, ALU.mult))
            step(dve.tensor_tensor(gates[:, n, 0], gates[:, n, 0], gates[:, n, 1], ALU.add))
            assert count[0] == GATE_STEPS
            dve.scalar_tensor_tensor(out=lora[:, n].rearrange("p (e r) -> p e r", r=RANK),
                                     in0=bank[4 + n][:, EXPERTS:GL].rearrange("p (e r) -> p e r", r=RANK),
                                     scalar=LORA / FSCALE, in1=gates[:, n, 0].unsqueeze(2).broadcast_to([P, EXPERTS, RANK]),
                                     op0=ALU.mult, op1=ALU.mult).then_inc(lora_gated, 1)

        def lora_low(t, n):
            dve.wait_ge(loraT_hi, t + 1)
            dve.tensor_tensor(loraT[:, n, 1], bank[6 + n][0:EH, 0:2 * P].rearrange("p (h t) -> p h t", h=2),
                              loraT[:, n, 0], ALU.subtract).then_inc(loraT_ready, 1)

        def finish(t, r, n, first):
            dve.wait_ge(ffn_psum, t + 1)
            if not first:
                dve.wait_ge(out_stored[n], 16 * r)
            dve.scalar_tensor_tensor(out=res[:, n], in0=bank[2 + n][:], scalar=1 / FSCALE, in1=tile_of(t),
                                     op0=ALU.mult, op1=ALU.add).then_inc(res_done, 1)

        def body(t, r, n, first, second, last):
            gate(t, n, last)
            if n == 1:
                finish(t - 1, r, 0, first)
            elif not first:
                finish(t - 1, r - 1, 1, second)
            lora_low(t, n)

        def split_low(k):
            dst, src = splits[k]
            dve.wait_ge(w_his, k + 1)
            dve.scalar_tensor_tensor(out=dst[:, 1], in0=src, scalar=FSCALE, in1=dst[:, 0], op0=ALU.mult,
                                     op1=ALU.subtract).then_inc(w_ready, 1)

        split_low(0)
        split_low(1)
        add_bias(0, 0)
        for k in range(2, len(splits)):
            split_low(k)
        dve.wait_ge(w_loaded, 16 * 2)
        for n in range(2):
            body(n, 0, n, True, False, False)
        for n in range(2):
            body(2 + n, 1, n, False, True, False)
        with dve.Fori(2, ROUNDS - 1) as r:
            for n in range(2):
                body(2 * r + n, r, n, False, False, False)
        for n in range(2):
            body(TILES - 2 + n, ROUNDS - 1, n, False, False, n == 1)
        finish(TILES - 1, ROUNDS - 1, 1, False)


def kernel(**inputs):
    import numpy as np
    import concourse.bacc as bacc
    from concourse.bass_utils import run_bass_kernel_spmd

    i = {k: np.asarray(v) for k, v in inputs.items()}

    def cols(codes, perm=None):
        n = codes.shape[1] // NKV
        return codes.reshape(KT, P, NKV, n).transpose(2, 1, 0, 3).reshape(NKV, P, KT * n)

    def split_dims(m, heads):
        rows = m.shape[0]
        if heads == NKV:
            return m.reshape(rows, NKV, HD // 2, 2).transpose(0, 1, 3, 2).reshape(rows, -1)
        return m.reshape(rows, NKV * 2, 2, HD // 2, 2).transpose(0, 1, 4, 2, 3).reshape(rows, -1)

    def by_step(*parts):
        w = np.concatenate(parts, axis=2)
        rows = w.shape[1]
        return w.reshape(NKV, rows, STEPS_G, -1).transpose(0, 2, 1, 3).reshape(TILES, rows, -1)

    codes = np.concatenate([
        by_step(cols(split_dims(i["L0_attn_q_codes"], 32))),
        by_step(cols(split_dims(i["L0_attn_k_codes"], NKV)), cols(i["L0_attn_v_codes"]),
                i["L0_attn_o_codes"].reshape(NKV, RF, P, D).transpose(0, 2, 1, 3).reshape(NKV, P, RF * D))], axis=2)

    def srow(s):
        n = s.shape[1] // NKV
        return s.reshape(KT, NKV, n).transpose(1, 0, 2).reshape(NKV, 1, KT * n)

    scales = by_step(srow(split_dims(i["L0_attn_k_scales"], NKV)),
                     srow(i["L0_attn_v_scales"]), i["L0_attn_o_scales"].reshape(NKV, 1, RF * D))[:, 0]

    inv_freq = (1.0 / np.float32(10000.0) ** (np.arange(0, HD, 2, dtype=np.float32) / np.float32(HD))).astype(np.float32)
    f = np.arange(S, dtype=np.float32)[None, :] * inv_freq[:, None]
    cos, sin = np.cos(f), np.sin(f)
    conv_w = np.zeros((S, TAPS, S), np.float32)
    for g in range(CGROUPS):
        rows = slice(CG * g, CG * (g + 1))
        conv_w[rows, :, rows] = i["L0_cond_weight"][rows].transpose(1, 2, 0)
    t, s = np.arange(S)[:, None], np.arange(S)[None, :]
    arrays = {
        "x": i["x"].reshape(TOKENS, D),
        "conv_w": conv_w,
        "params": np.concatenate([
            i["cond_128"].T, i["L0_cond2_W0"], i["L0_cond2_b0"].reshape(P, 1), i["L0_cond_c_weight"].T,
            np.broadcast_to(i["fside_S_0"].reshape(1, S), (P, S)), i["L0_cond2_W1"], np.eye(P, dtype=np.float32),
            i["L0_cond2_b1"].reshape(P, 1), i["L0_cond2_W2"],
            np.broadcast_to(i["L0_cond2_b2"].reshape(1, COND_K), (P, COND_K))], axis=1),
        "kern": np.concatenate([i["L0_cond2_weight"].reshape(COND_K, S, S).transpose(0, 2, 1).reshape(COND_K, S * S),
                                i["L0_cond2_bias_k"].reshape(COND_K, S)], axis=1),
        "codes": codes,
        "scales": scales,
        "base_T": i["L0_ffn_base_W"].T.reshape(KT, P, D).transpose(1, 0, 2),
        "gl_T": np.concatenate([i["L0_ffn_gate_W"].T, i["L0_ffn_lora_A"].reshape(ER, D).T], axis=1)
        .reshape(KT, P, GL).transpose(1, 0, 2),
        "lb_T": i["L0_ffn_lora_B"].transpose(0, 2, 1).reshape(2, EH, D).transpose(1, 0, 2),
        "ident": np.eye(P, dtype=np.float32),
        "iota": np.arange(EXPERTS, dtype=np.float32),
        "cos2": np.concatenate([cos, cos]),
        "sin2": np.concatenate([sin, sin]),
        "cos_k": np.concatenate([cos, cos]) / np.float32(WSCALE),
        "sin_k": np.concatenate([sin, -sin]) / np.float32(WSCALE),
        "q_scales": split_dims(i["L0_attn_q_scales"], 32).reshape(KT, NKV, 2 * 2, P).transpose(3, 1, 2, 0),
        "mask": np.tile(np.where(t > s, np.float32(-1e30), np.float32(0)), (TB, 1)),
    }
    arrays = {k: np.ascontiguousarray(v) for k, v in arrays.items()}
    nc = bacc.Bacc("TRN2", target_bir_lowering=False, num_devices=1)
    aps = {k: nc.dram_tensor(f"in_{k}", v.shape, mybir.dt.from_np(v.dtype), kind="ExternalInput").ap()
           for k, v in arrays.items()}
    out = nc.dram_tensor("out", [TOKENS, D], F32, kind="ExternalOutput").ap()
    layer(nc, aps, out)
    r = run_bass_kernel_spmd(nc, [{f"in_{k}": v for k, v in arrays.items()}], core_ids=[0])
    return r.results[0]["out"].reshape(B, S, D)
```
